# Optimizing a Trainium2 kernel written in Bass

```python
import numpy as np
import jax
import jax.numpy as jnp

def _softmax(x, axis=-1):
    return jax.nn.softmax(x, axis=axis)

def _gelu(x):
    return jax.nn.gelu(x, approximate=True)

def _silu(x):
    return jax.nn.silu(x)

def _sigmoid(x):
    return jax.nn.sigmoid(x)

def _layernorm(x, axis=-1, eps=1e-05):
    m = jnp.mean(x, axis=axis, keepdims=True)
    v = jnp.var(x, axis=axis, keepdims=True)
    return (x - m) / jnp.sqrt(v + eps)

def _scatter_add(tgt, idx, src, axis=0):
    return tgt.at[idx].add(src)

def _segment_sum(src, seg, n):
    return jax.ops.segment_sum(src, seg, n)
kernel_name = 'mk_flamingo_gated_d1_seqx_r2_ededd4'

def setup_inputs(seed: int=0):
    np.random.seed(seed)
    _w = jnp.asarray

    def _rec_inputs():
        import jax
        import jax.numpy as jnp
        _rk = jax.random.key(seed)
        x = -0.0003929 + 0.9999 * jax.random.normal(jax.random.fold_in(_rk, 1), (64, 512, 512), jnp.float32)
        _lenS = 512 - jax.random.randint(jax.random.fold_in(_rk, 7), (64,), 0, max(1, 512 // 4) + 1, jnp.int32)
        _lenS2 = 77 - jax.random.randint(jax.random.fold_in(_rk, 8), (64,), 0, max(1, 77 // 4) + 1, jnp.int32)
        _ctx_2048P = jax.random.normal(jax.random.fold_in(_rk, 11), (64, 16, 1024), jnp.float32)
        _ctx_2048c = jax.random.dirichlet(jax.random.fold_in(_rk, 511), 0.3 * jnp.ones((16,), jnp.float32), (64, 77))
        _ctx_2048t = jnp.einsum('bsk,bkd->bsd', _ctx_2048c, _ctx_2048P)
        _ctx_2048t = _ctx_2048t * jax.lax.rsqrt(jnp.mean(jnp.square(_ctx_2048t)) + 1e-12) * 0.953939
        ctx_2048 = 4.13588e-05 + 0.999923 * (_ctx_2048t + 0.3 * jax.random.normal(jax.random.fold_in(_rk, 611), (64, 77, 1024), jnp.float32))
        _validS = jnp.arange(512)[None, :] < _lenS[:, None]
        _validS2 = jnp.arange(77)[None, :] < _lenS2[:, None]
        _causal = jnp.tril(jnp.ones((512, 512), dtype=bool))
        mask_BxS2_if0 = jnp.where(jnp.ones((64, 77), dtype=bool), 4, 0).astype(jnp.int32)
        _g = jax.random.normal(jax.random.fold_in(_rk, 9001), (2, 1), jnp.float32)
        _g = jnp.sign(_g) * jnp.maximum(jnp.abs(_g), 1.0) + (_g == 0) * 1.0
        g_xattn = _g[0]
        g_ffn = _g[1]
        return (x, ctx_2048, mask_BxS2_if0, g_xattn, g_ffn)
    x, ctx_2048, mask_BxS2_if0, g_xattn, g_ffn = _rec_inputs()

    def _L0_xattn_setup():
        import jax, jax.numpy as jnp
        import numpy as np
        B, L, P = (4, 2048, 512)
        D_MODEL = 512
        D_GLOBAL = 1024
        HEADDIM = 32
        EPSILON = 0.001
        RMS_EPS = 1e-05

        def rmsnorm(x, g, eps=RMS_EPS):
            var = jnp.mean(jnp.square(x), axis=-1, keepdims=True)
            return x * jax.lax.rsqrt(var + eps) * g

        def _hnet_depool(h, h_patch_full, patch_lens):
            h_patch = h_patch_full[..., :D_MODEL]
            bsz, plen = (h_patch.shape[0], h_patch.shape[1])
            seqlen = h.shape[1]
            logp = jnp.full((bsz, plen), -EPSILON, dtype=jnp.float32)
            bidx = jnp.cumsum(patch_lens, axis=1) - 1
            boundary_mask = jnp.zeros((bsz, seqlen), dtype=jnp.int32)
            boundary_mask = boundary_mask.at[jnp.arange(bsz)[:, None], bidx].set(1)
            dt = (-jnp.log(-jnp.expm1(logp))).astype(h_patch.dtype)
            x = h_patch / dt[..., None]
            n_heads = D_MODEL // HEADDIM
            A = -jnp.ones((n_heads,), dtype=jnp.float32)
            bcoef = jnp.exp(logp).astype(h_patch.dtype)
            x4 = x.reshape(bsz, plen, n_heads, HEADDIM)
            a = jnp.exp(dt[:, :, None] * A[None, None, :])
            u = (dt * bcoef)[:, :, None, None] * x4
            a_b = jnp.broadcast_to(a[..., None], u.shape)

            def comb(lft, rgt):
                aL, uL = lft
                aR, uR = rgt
                return (aL * aR, uL * aR + uR)
            _, s = jax.lax.associative_scan(comb, (a_b, u), axis=1)
            depool = s.reshape(bsz, plen, D_MODEL)
            plug = jnp.clip(jnp.cumsum(boundary_mask, axis=1) - 1, 0, plen - 1)
            depool_out = depool[jnp.arange(bsz)[:, None], plug]
            return depool_out + h
        key = jax.random.key(seed)
        k1, k2, k3, k4 = jax.random.split(key, 4)
        embeds = jax.random.normal(k1, (B, L, D_MODEL), dtype=jnp.float32)
        patch_embeds = jax.random.normal(k2, (B, P, D_GLOBAL), dtype=jnp.float32)
        patch_lens = jnp.full((B, P), L // P, dtype=jnp.int64)
        W_in = jax.random.normal(k3, (D_MODEL, D_MODEL), dtype=jnp.float32) * 0.02
        b_in = jnp.zeros((D_MODEL,), dtype=jnp.float32)
        g_res = jnp.ones((D_MODEL,), dtype=jnp.float32)
        g_init = jnp.ones((D_GLOBAL,), dtype=jnp.float32)
        return {'embeds': embeds, 'patch_embeds': patch_embeds, 'patch_lens': patch_lens, 'W_in': W_in, 'b_in': b_in, 'g_res': g_res, 'g_init': g_init}
    _L0_xattn_all = _L0_xattn_setup()
    _L0_xattn_in = {k: v for k, v in _L0_xattn_all.items() if k in ('W_in', 'b_in', 'g_res', 'g_init')}
    del _L0_xattn_all

    def _L0_ffn_setup():
        import jax, jax.numpy as jnp
        import numpy as np
        B, T = (2, 1024)
        D_MODEL, D_HIDDEN = (512, 1024)
        N_EXPERTS, TOP_K = (8, 2)
        N_TOKENS = B * T
        CAPACITY = 2 * N_TOKENS * TOP_K // N_EXPERTS
        key = jax.random.key(seed)
        k_x, k_rw, k_w, k_v, k_o = jax.random.split(key, 5)
        x = jax.random.normal(k_x, (B, T, D_MODEL), jnp.float32)
        router_w = jax.random.normal(k_rw, (N_EXPERTS, D_MODEL), jnp.float32) * D_MODEL ** (-0.5)
        router_b = jnp.zeros((N_EXPERTS,), jnp.float32)
        W = jax.random.normal(k_w, (N_EXPERTS, D_MODEL, D_HIDDEN), jnp.float32) * D_MODEL ** (-0.5)
        V = jax.random.normal(k_v, (N_EXPERTS, D_MODEL, D_HIDDEN), jnp.float32) * D_MODEL ** (-0.5)
        W_out = jax.random.normal(k_o, (N_EXPERTS, D_HIDDEN, D_MODEL), jnp.float32) * D_HIDDEN ** (-0.5)
        return {'x': x, 'router_w': router_w, 'router_b': router_b, 'W': W, 'V': V, 'W_out': W_out}
    _L0_ffn_all = _L0_ffn_setup()
    _L0_ffn_in = {k: v for k, v in _L0_ffn_all.items() if k in ('router_w', 'router_b', 'W', 'V', 'W_out')}
    del _L0_ffn_all
    return {'x': x, 'ctx_2048': ctx_2048, 'mask_BxS2_if0': mask_BxS2_if0, 'g_xattn': g_xattn, 'g_ffn': g_ffn, 'L0_xattn_W_in': _L0_xattn_in['W_in'], 'L0_xattn_b_in': _L0_xattn_in['b_in'], 'L0_xattn_g_res': _L0_xattn_in['g_res'], 'L0_xattn_g_init': _L0_xattn_in['g_init'], 'L0_ffn_router_w': _L0_ffn_in['router_w'], 'L0_ffn_router_b': _L0_ffn_in['router_b'], 'L0_ffn_W': _L0_ffn_in['W'], 'L0_ffn_V': _L0_ffn_in['V'], 'L0_ffn_W_out': _L0_ffn_in['W_out']}

def reference(x, ctx_2048, mask_BxS2_if0, g_xattn, g_ffn, L0_xattn_W_in, L0_xattn_b_in, L0_xattn_g_res, L0_xattn_g_init, L0_ffn_router_w, L0_ffn_router_b, L0_ffn_W, L0_ffn_V, L0_ffn_W_out):
    import jax
    import jax.numpy as jnp

    def _L0_xattn_ref(embeds, patch_embeds, patch_lens, W_in, b_in, g_res, g_init):
        import jax, jax.numpy as jnp
        import numpy as np
        B, L, P = (4, 2048, 512)
        D_MODEL = 512
        D_GLOBAL = 1024
        HEADDIM = 32
        EPSILON = 0.001
        RMS_EPS = 1e-05

        def rmsnorm(x, g, eps=RMS_EPS):
            var = jnp.mean(jnp.square(x), axis=-1, keepdims=True)
            return x * jax.lax.rsqrt(var + eps) * g

        def _hnet_depool(h, h_patch_full, patch_lens):
            h_patch = h_patch_full[..., :D_MODEL]
            bsz, plen = (h_patch.shape[0], h_patch.shape[1])
            seqlen = h.shape[1]
            logp = jnp.full((bsz, plen), -EPSILON, dtype=jnp.float32)
            bidx = jnp.cumsum(patch_lens, axis=1) - 1
            boundary_mask = jnp.zeros((bsz, seqlen), dtype=jnp.int32)
            boundary_mask = boundary_mask.at[jnp.arange(bsz)[:, None], bidx].set(1)
            dt = (-jnp.log(-jnp.expm1(logp))).astype(h_patch.dtype)
            x = h_patch / dt[..., None]
            n_heads = D_MODEL // HEADDIM
            A = -jnp.ones((n_heads,), dtype=jnp.float32)
            bcoef = jnp.exp(logp).astype(h_patch.dtype)
            x4 = x.reshape(bsz, plen, n_heads, HEADDIM)
            a = jnp.exp(dt[:, :, None] * A[None, None, :])
            u = (dt * bcoef)[:, :, None, None] * x4
            a_b = jnp.broadcast_to(a[..., None], u.shape)

            def comb(lft, rgt):
                aL, uL = lft
                aR, uR = rgt
                return (aL * aR, uL * aR + uR)
            _, s = jax.lax.associative_scan(comb, (a_b, u), axis=1)
            depool = s.reshape(bsz, plen, D_MODEL)
            plug = jnp.clip(jnp.cumsum(boundary_mask, axis=1) - 1, 0, plen - 1)
            depool_out = depool[jnp.arange(bsz)[:, None], plug]
            return depool_out + h
        h = rmsnorm(embeds, g_res)
        h = jnp.einsum('bld,ed->ble', h, W_in) + b_in
        h_patch = rmsnorm(patch_embeds, g_init)
        return _hnet_depool(h, h_patch, patch_lens)

    def _L0_ffn_ref(x, router_w, router_b, W, V, W_out):
        import jax, jax.numpy as jnp
        import numpy as np
        B, T = (2, 1024)
        D_MODEL, D_HIDDEN = (512, 1024)
        N_EXPERTS, TOP_K = (8, 2)
        N_TOKENS = B * T
        CAPACITY = 2 * N_TOKENS * TOP_K // N_EXPERTS
        Bq, Tq, D = x.shape
        N = Bq * Tq
        x_flat = x.reshape(N, D)
        router_logits = x_flat @ router_w.T + router_b
        top_vals, top_ids = jax.lax.top_k(router_logits, TOP_K)
        top_probs = jax.nn.softmax(top_vals, axis=-1)
        x_pad = jnp.concatenate([x_flat, jnp.zeros((1, D), x_flat.dtype)], axis=0)
        probs_pad = jnp.concatenate([top_probs, jnp.zeros((1, TOP_K), top_probs.dtype)], axis=0)
        out = jnp.zeros((N + 1, D), x_flat.dtype)
        for e in range(N_EXPERTS):
            tok, slot = jnp.nonzero(top_ids == e, size=CAPACITY, fill_value=(N, 0))
            w = probs_pad[tok, slot][:, None]
            xin = x_pad[tok]
            a = xin @ W[e]
            b = xin @ V[e]
            y = a * (b * jax.nn.sigmoid(b)) @ W_out[e]
            out = out.at[tok].add(y * w)
        return out[:N].reshape(Bq, Tq, D)
    x = x + jnp.tanh(g_xattn[0]) * _L0_xattn_ref(_layernorm(x, axis=-1), ctx_2048, mask_BxS2_if0, L0_xattn_W_in, L0_xattn_b_in, L0_xattn_g_res, L0_xattn_g_init)
    x = x + jnp.tanh(g_ffn[0]) * _L0_ffn_ref(_layernorm(x, axis=-1), L0_ffn_router_w, L0_ffn_router_b, L0_ffn_W, L0_ffn_V, L0_ffn_W_out)
    return x

_drawn_inputs = setup_inputs


def setup_inputs(seed=0):
    import zlib

    import numpy as np

    out = dict(_drawn_inputs(seed))
    spreads = {'L0_xattn_b_in': (0.0, 0.1),
     'L0_xattn_g_res': (1.0, 0.2),
     'L0_xattn_g_init': (1.0, 0.2),
     'L0_ffn_router_b': (0.0, 0.1)}
    factors = {}
    for name, (base, spread) in spreads.items():
        noise = np.random.default_rng([zlib.crc32(name.encode()), seed]).standard_normal(out[name].shape)
        drawn = base * np.exp(spread * noise) if base else spread * noise
        out[name] = jnp.asarray(drawn.astype(out[name].dtype))
    for name, factor in factors.items():
        out[name] = (out[name] * factor).astype(out[name].dtype)
    return out
```

```python
from contextlib import ExitStack

import numpy as np
import concourse.bass as bass
from concourse import mybir

F32 = mybir.dt.float32
F32R = mybir.dt.float32r
F16 = mybir.dt.float16
I32 = mybir.dt.int32
U32 = mybir.dt.uint32
ALU = mybir.AluOpType
ACT = mybir.ActivationFunctionType
AX_X = mybir.AxisListType.X

P = 128
BATCH, SEQ, D = 64, 512, 512
TOKENS = BATCH * SEQ
PATCHES, D_CTX = 77, 1024
HIDDEN, EXPERTS, TOP_K = 1024, 8, 2
CAPACITY = 2 * 2048 * TOP_K // EXPERTS
EPS = 1e-5
KC = D // P
TPB = SEQ // P
HC = HIDDEN // P
ET = CAPACITY // P
ROWS = PATCHES + 1
GROUP = 4
RT = 8
FAR = 32768
DMA = 16

_LOGP = np.float32(-0.001)
_DT = -np.log(-np.expm1(_LOGP.astype(np.float64)))


def wait_count(eng, sem, count):
    if not isinstance(count, int) or count > 0:
        eng.wait_ge(sem, count)


def hold(eng, sem, count, passed):
    eng.wait_ge(sem, count)
    eng.sem_inc(passed)


def constants():
    decay = np.zeros((ROWS, ROWS))
    q, p = np.meshgrid(np.arange(PATCHES), np.arange(PATCHES))
    decay[:PATCHES, :PATCHES] = np.where(q >= p, np.exp(_LOGP) * np.exp(-_DT * np.maximum(q - p, 0)), 0.0)
    decay[PATCHES, PATCHES] = 1.0
    at = np.arange(P)
    select = np.zeros((PATCHES, 2 * P), np.float16)
    select[:, P] = 1.0
    fill = np.zeros((P, EXPERTS * ET, 2), np.int32)
    fill[:, :, 0] = TOKENS
    return {
        "c_eye": np.eye(P, dtype=np.float32),
        "c_decay": decay.astype(np.float32),
        "c_prefix": (np.arange(PATCHES)[:, None] <= np.arange(PATCHES)[None, :]).astype(np.float32),
        "c_rank": np.arange(1, PATCHES + 1, dtype=np.float32)[:, None],
        "c_pos": np.broadcast_to(np.arange(SEQ, dtype=np.float16), (PATCHES, SEQ)),
        "c_select": select,
        "c_before": (at[:, None] < at[None, :]).astype(np.float16),
        "c_expert": np.broadcast_to(np.arange(EXPERTS, dtype=np.float32), (P, EXPERTS)),
        "c_token": (np.arange(RT)[None, :] * P + at[:, None]).astype(np.float32),
        "c_fill": fill.reshape(P, -1),
    }


def mix(nc, io, x1_dram, tokens_dram):
    with ExitStack() as ctx:
        def sb(name, shape, dt=F32):
            return ctx.enter_context(nc.sbuf_tensor(name, shape, dt))

        def ps(name, shape):
            return ctx.enter_context(nc.psum_tensor(name, shape, F32))

        def sem(name):
            return ctx.enter_context(nc.semaphore(name))

        eye = sb("eye", [P, P])
        decay = sb("decay", [ROWS, ROWS])
        prefix = sb("prefix", [PATCHES, PATCHES])
        rank = sb("rank", [PATCHES, 1])
        pos = sb("pos", [PATCHES, SEQ], F16)
        select = sb("select", [PATCHES, 2 * P], F16)
        lens_i = sb("lens_i", [PATCHES, BATCH], I32)
        lens = sb("lens", [PATCHES, BATCH])
        ends = sb("ends", [PATCHES, BATCH])
        wraps = sb("wraps", [PATCHES, BATCH])
        gate_in = sb("gate_in", [P, 1])
        gate = sb("gate", [P, 1])
        gain_res = sb("gain_res", [P, KC])
        gain_ctx = sb("gain_ctx", [PATCHES, D])
        half = sb("half", [P, 5])
        zeros = sb("zeros", [P, D])
        w_raw = sb("w_raw", [P, KC, D])
        w_hi = sb("w_hi", [P, KC, D], F32R)
        w_lo = sb("w_lo", [P, KC, D], F32R)
        is_end = [sb(f"is_end{i}", [PATCHES, SEQ], F16) for i in range(4)]
        marks = sb("marks", [BATCH, SEQ])
        plug = sb("plug", [BATCH, SEQ], F16)
        x_in = [sb(f"x_in{i}", [P, TPB, D]) for i in range(GROUP)]
        c_in = [sb(f"c_in{i}", [PATCHES, D_CTX]) for i in range(GROUP)]
        p_in = [sb(f"p_in{i}", [PATCHES, SEQ], F16) for i in range(GROUP)]
        x1 = [sb(f"x1_{i}", [P, TPB, D]) for i in range(2)]
        tile_stats = [sb(f"tile_stats{i}", [P, TPB, 6]) for i in range(2)]
        moments = [sb(f"moments{i}", [P, TPB, 2]) for i in range(2)]
        spread = [sb(f"spread{i}", [P, 5]) for i in range(2)]
        scale = [sb(f"scale{i}", [P, 5]) for i in range(2)]
        shift = [sb(f"shift{i}", [P, TPB]) for i in range(2)]
        squares = sb("squares", [PATCHES, D_CTX])
        sumsq = [sb(f"sumsq{i}", [PATCHES, 1]) for i in range(2)]
        patch = [sb(f"patch{i}", [ROWS, D]) for i in range(2)]
        pool_hi = [sb(f"pool_hi{i}", [ROWS, D], F32R) for i in range(2)]
        pool_lo = [sb(f"pool_lo{i}", [ROWS, D], F32R) for i in range(2)]
        onehot = [sb(f"onehot{i}", [ROWS, SEQ], F32R) for i in range(2)]
        xn = [sb(f"xn{i}", [P, D]) for i in range(2)]
        xt_hi = [sb(f"xt_hi{i}", [P, D], F32R) for i in range(2)]
        xt_lo = [sb(f"xt_lo{i}", [P, D], F32R) for i in range(2)]

        ps_t = [ps(f"ps_t{i}", [P, D]) for i in range(2)]
        ps_o = [ps(f"ps_o{i}", [P, D]) for i in range(2)]
        ps_d = ps("ps_d", [P, D])
        ps_c = ps("ps_c", [P, SEQ])

        const_loaded = sem("const_loaded")
        plug_stored = sem("plug_stored")
        tokens_cleared = sem("tokens_cleared")
        batch_loaded = [sem(f"batch_loaded{i}") for i in range(GROUP)]
        x1_stored = [sem(f"x1_stored{i}") for i in range(2)]
        const_set = sem("const_set")
        prep = sem("prep")
        ends_summed = sem("ends_summed")
        end_marked = sem("end_marked")
        end_added = sem("end_added")
        plug_ready = sem("plug_ready")
        w_scaled = sem("w_scaled")
        w_hi_ready = sem("w_hi_ready")
        w_lo_ready = sem("w_lo_ready")
        gate_ready = sem("gate_ready")
        stats_done = sem("stats_done")
        moments_done = sem("moments_done")
        sumsq_ready = sem("sumsq_ready")
        spread_ready = sem("spread_ready")
        scale_ready = sem("scale_ready")
        shift_ready = sem("shift_ready")
        normed = sem("normed")
        turned = sem("turned")
        hi_ready = sem("hi_ready")
        lo_ready = sem("lo_ready")
        mixed = sem("mixed")
        x1_ready = sem("x1_ready")
        patch_ready = sem("patch_ready")
        pooled = sem("pooled")
        pool_hi_ready = sem("pool_hi_ready")
        pool_lo_ready = sem("pool_lo_ready")
        onehot_ready = sem("onehot_ready")
        passed = sem("passed_mix")

        plug_dram = nc.dram_tensor("plug_dram", [BATCH, SEQ], F16, kind="Internal").ap()
        LOADS = [
            (lens_i, io["lens"]), (prefix, io["c_prefix"]), (pos, io["c_pos"]), (select, io["c_select"]),
            (eye, io["c_eye"]), (decay, io["c_decay"]), (rank, io["c_rank"]),
            (gain_res, io["gain_res"]), (gain_ctx, io["gain_ctx"][0:D].partition_broadcast(PATCHES)),
            (gate_in, io["g_xattn"].partition_broadcast(P)),
            (w_raw, io["w_in"].rearrange("(c p) e -> p c e", p=P)),
        ]
        CONSTS = DMA * (len(LOADS) + 2)
        LAST = BATCH // GROUP - 1

        with nc.Block() as block:

            @block.sync
            def _(eng):
                for dst, src in LOADS:
                    eng.dma_start(dst[:], src).then_inc(const_loaded, DMA)
                eng.wait_ge(const_set, 4)
                for i in range(2):
                    eng.dma_start(patch[i][PATCHES:ROWS, :], io["b_in"]).then_inc(const_loaded, DMA)

                def load(b, k):
                    eng.dma_start(x_in[k][:], io["x"][b].rearrange("(t p) d -> p t d", p=P)).then_inc(batch_loaded[k], DMA)
                    eng.dma_start(c_in[k][:], io["ctx"][b]).then_inc(batch_loaded[k], DMA)
                    eng.dma_start(p_in[k][:], plug_dram[b].partition_broadcast(PATCHES)).then_inc(batch_loaded[k], DMA)

                eng.wait_ge(plug_ready, 1)
                eng.dma_start(plug_dram, plug[:]).then_inc(plug_stored, DMA)
                eng.wait_ge(plug_stored, DMA)
                for k in range(GROUP):
                    load(k, k)
                eng.dma_start(tokens_dram.rearrange("(n p) d -> p n d", p=P),
                              zeros[:].unsqueeze(1).broadcast_to([P, EXPERTS * ET, D])).then_inc(tokens_cleared, DMA)

                def turn(g, last=False):
                    for k in range(GROUP):
                        b = GROUP * g + k
                        eng.wait_ge(x1_ready, TPB * (b + 1))
                        eng.dma_start(x1_dram[b].rearrange("(t p) d -> p t d", p=P), x1[k % 2][:]).then_inc(x1_stored[k % 2], DMA)
                        if not last:
                            load(b + GROUP, k)

                turn(0)
                with eng.Fori(1, LAST) as g:
                    turn(g)
                turn(LAST, last=True)
                for i in range(2):
                    eng.wait_ge(x1_stored[i], DMA * (BATCH // 2))
                eng.wait_ge(tokens_cleared, DMA)

            @block.gpsimd
            def _(eng):
                def root(b, k):
                    eng.wait_ge(spread_ready, 2 * (b + 1))
                    eng.tensor_tensor(scale[k % 2][:], spread[k % 2][:], half[:], ALU.pow).then_inc(scale_ready, 1)

                eng.wait_ge(const_set, 4)
                root(0, 0)

                def turn(g, last=False):
                    for k in range(GROUP):
                        if not (last and k == GROUP - 1):
                            root(GROUP * g + k + 1, (k + 1) % GROUP)

                turn(0)
                with eng.Fori(1, LAST) as g:
                    turn(g)
                turn(LAST, last=True)

            @block.tensor
            def _(eng):
                eng.wait_ge(prep, 1)
                eng.matmul(ps_c[0:PATCHES, 0:BATCH], prefix[:], lens[:], start=True, stop=True).then_inc(ends_summed, 1)

                def add_marks(b, k, first=False, last=False):
                    hold(eng, end_marked, b + 1, passed)
                    eng.matmul(ps_o[0][:], select[:, bass.ds(P - b, P)], is_end[k][:], start=first, stop=last,
                               skip_group_check=True).then_inc(end_added, 1)

                for k in range(4):
                    add_marks(k, k, first=k == 0)
                with eng.Fori(1, BATCH // 4 - 1) as g:
                    for k in range(4):
                        add_marks(4 * g + k, k)
                for k in range(4):
                    add_marks(BATCH - 4 + k, k, last=k == 3)

                def turn_tile(n, j):
                    eng.wait_ge(normed, n + 1)
                    wait_count(eng, hi_ready, n - 1)
                    wait_count(eng, lo_ready, n - 1)
                    for c in range(KC):
                        mm = eng.transpose(ps_t[j][:, c * P:(c + 1) * P], xn[j][:, c * P:(c + 1) * P], eye[:])
                    mm.then_inc(turned, 1)

                def depool(b, k):
                    eng.wait_ge(patch_ready, b + 1)
                    wait_count(eng, pool_hi_ready, b)
                    wait_count(eng, pool_lo_ready, b)
                    eng.matmul(ps_d[0:ROWS, :], decay[:], patch[k % 2][:], start=True, stop=True).then_inc(pooled, 1)

                def mix_tile(n, b, k, t):
                    j = t % 2
                    eng.wait_ge(hi_ready, n + 1)
                    eng.wait_ge(lo_ready, n + 1)
                    wait_count(eng, x1_ready, n - 1)
                    for c in range(KC):
                        own = slice(c * P, (c + 1) * P)
                        eng.matmul(ps_o[j][:], xt_hi[j][:, own], w_hi[:, c, :], start=c == 0, stop=False)
                        eng.matmul(ps_o[j][:], xt_hi[j][:, own], w_lo[:, c, :], start=False, stop=False)
                        eng.matmul(ps_o[j][:], xt_lo[j][:, own], w_hi[:, c, :], start=False, stop=False)
                    if t == 0:
                        eng.wait_ge(onehot_ready, b + 1)
                        eng.wait_ge(pool_hi_ready, b + 1)
                        eng.wait_ge(pool_lo_ready, b + 1)
                    own = slice(t * P, (t + 1) * P)
                    eng.matmul(ps_o[j][:], onehot[k % 2][:, own], pool_hi[k % 2][:], start=False, stop=False)
                    eng.matmul(ps_o[j][:], onehot[k % 2][:, own], pool_lo[k % 2][:], start=False, stop=True).then_inc(mixed, 1)

                eng.wait_ge(const_loaded, CONSTS)
                depool(0, 0)
                turn_tile(0, 0)
                eng.wait_ge(w_hi_ready, 1)
                eng.wait_ge(w_lo_ready, KC)
                eng.wait_ge(plug_ready, 1)

                def turn(g, last=False):
                    for k in range(GROUP):
                        b = GROUP * g + k
                        end = last and k == GROUP - 1
                        for t in range(TPB):
                            n = TPB * b + t
                            if not (end and t == TPB - 1):
                                turn_tile(n + 1, (t + 1) % 2)
                            if t == TPB - 1 and not end:
                                depool(b + 1, k + 1)
                            mix_tile(n, b, k, t)

                turn(0)
                with eng.Fori(1, LAST) as g:
                    turn(g)
                turn(LAST, last=True)

            @block.scalar
            def _(eng):
                def square_row(row, turn_no, k):
                    eng.wait_ge(batch_loaded[k], 3 * DMA * turn_no)
                    wait_count(eng, spread_ready, 2 * row - 2)
                    eng.activation(squares[:], c_in[k][:], ACT.Square, accum_out=sumsq[k % 2][:]).then_inc(sumsq_ready, 1)

                def norm_tile(n, row, k, t):
                    if t == 0:
                        eng.wait_ge(shift_ready, row + 1)
                    wait_count(eng, turned, n - 1)
                    eng.activation(xn[t % 2][:], x_in[k][:, t, :], ACT.Identity, bias=shift[k % 2][:, t:t + 1],
                                   scale=scale[k % 2][:, t:t + 1]).then_inc(normed, 1)

                def hi_tile(n, j):
                    eng.wait_ge(turned, n + 1)
                    wait_count(eng, mixed, n - 1)
                    eng.activation(xt_hi[j][:], ps_t[j][:], ACT.Copy).then_inc(hi_ready, 1)

                def hi_pool(row, k):
                    eng.wait_ge(pooled, row + 1)
                    wait_count(eng, mixed, TPB * (row - 1))
                    eng.activation(pool_hi[k % 2][:], ps_d[0:ROWS, :], ACT.Copy).then_inc(pool_hi_ready, 1)

                eng.wait_ge(const_loaded, CONSTS)
                eng.activation(gate[:], gate_in[:], ACT.Tanh).then_inc(gate_ready, 1)
                eng.wait_ge(w_scaled, KC)
                eng.activation(w_hi[:], w_raw[:], ACT.Copy).then_inc(w_hi_ready, 1)
                square_row(0, 1, 0)
                norm_tile(0, 0, 0, 0)
                norm_tile(1, 0, 0, 1)
                hi_pool(0, 0)
                hi_tile(0, 0)

                def turn(g, last=False):
                    for k in range(GROUP):
                        b = GROUP * g + k
                        nk = (k + 1) % GROUP
                        end = last and k == GROUP - 1
                        for t in range(TPB):
                            n = TPB * b + t
                            if not (end and t == TPB - 1):
                                hi_tile(n + 1, (t + 1) % 2)
                            if t + 2 < TPB:
                                norm_tile(n + 2, b, k, t + 2)
                            elif not end:
                                norm_tile(n + 2, b + 1, nk, t + 2 - TPB)
                            if t == 0 and not end:
                                square_row(b + 1, g + 1 + (k + 1) // GROUP, nk)
                            if t == TPB - 1 and not end:
                                hi_pool(b + 1, nk)

                turn(0)
                with eng.Fori(1, LAST) as g:
                    turn(g)
                turn(LAST, last=True)

            @block.vector
            def _(eng):
                for i in range(2):
                    eng.memset(spread[i][:], 1.0)
                    eng.memset(onehot[i][:].bitcast(F32), 1.0).then_inc(const_set, 1)
                eng.memset(half[:], -0.5).then_inc(const_set, 1)
                eng.memset(zeros[:], 0.0)
                eng.memset(patch[0][:], 0.0)
                eng.memset(patch[1][:], 0.0).then_inc(const_set, 1)

                eng.wait_ge(const_loaded, CONSTS)
                eng.tensor_copy(lens[:], lens_i[:]).then_inc(prep, 1)
                eng.wait_ge(ends_summed, 1)
                eng.tensor_scalar(ends[:], ps_c[0:PATCHES, 0:BATCH], -1.0, None, ALU.add).then_inc(prep, 1)
                eng.wait_ge(prep, 2)
                eng.tensor_scalar(wraps[:], ends[:], 0.0, float(SEQ), ALU.is_lt, ALU.mult).then_inc(prep, 1)
                eng.wait_ge(prep, 3)
                eng.tensor_tensor(ends[:], ends[:], wraps[:], ALU.add).then_inc(prep, 1)
                eng.wait_ge(prep, 4)

                def mark(b, k):
                    wait_count(eng, end_added, b - 3)
                    eng.tensor_scalar(is_end[k][:], pos[:], ends[:, bass.ds(b, 1)], None, ALU.is_equal).then_inc(end_marked, 1)

                for k in range(4):
                    mark(k, k)
                with eng.Fori(1, BATCH // 4) as g:
                    for k in range(4):
                        mark(4 * g + k, k)
                eng.wait_ge(end_added, BATCH)
                eng.tensor_scalar(marks[:], ps_o[0][0:BATCH, :], 1.0, None, ALU.min).then_inc(prep, 1)
                eng.wait_ge(prep, 5)
                eng.tensor_tensor_scan(plug[:], marks[:], marks[:], 0.0, ALU.add, ALU.max).then_inc(plug_ready, 1)

                for c in range(KC):
                    eng.tensor_scalar(w_raw[:, c, :], w_raw[:, c, :], gain_res[:, c:c + 1], None, ALU.mult).then_inc(w_scaled, 1)
                eng.wait_ge(w_hi_ready, 1)
                for c in range(KC):
                    eng.tensor_tensor(w_lo[:, c, :], w_raw[:, c, :], w_hi[:, c, :].bitcast(F32), ALU.subtract).then_inc(w_lo_ready, 1)

                def stats(row, turn_no, k, tiles):
                    if tiles[0] == 0:
                        eng.wait_ge(batch_loaded[k], 3 * DMA * turn_no)
                    for t in tiles:
                        eng.bn_stats(tile_stats[k % 2][:, t, :], x_in[k][:, t, :]).then_inc(stats_done, 1)

                def spreads(row, k):
                    hold(eng, stats_done, TPB * (row + 1), passed)
                    for t in range(TPB):
                        eng.bn_aggr(moments[k % 2][:, t, :], tile_stats[k % 2][:, t, :]).then_inc(moments_done, 1)
                    eng.wait_ge(moments_done, TPB * (row + 1))
                    eng.tensor_scalar(spread[k % 2][:, 0:TPB], moments[k % 2][:, :, 1], 1.0 + EPS, EPS * EPS,
                                      ALU.mult, ALU.add).then_inc(spread_ready, 1)
                    eng.wait_ge(sumsq_ready, row + 1)
                    eng.tensor_scalar(spread[k % 2][0:PATCHES, TPB:TPB + 1], sumsq[k % 2][:], 1.0 / D_CTX, EPS,
                                      ALU.mult, ALU.add).then_inc(spread_ready, 1)

                def shifts(row, k):
                    eng.wait_ge(scale_ready, row + 1)
                    eng.scalar_tensor_tensor(shift[k % 2][:], moments[k % 2][:, :, 0], -1.0, scale[k % 2][:, 0:TPB],
                                             ALU.mult, ALU.mult).then_inc(shift_ready, 1)

                def patches(row, k):
                    wait_count(eng, pooled, row - 1)
                    eng.scalar_tensor_tensor(patch[k % 2][0:PATCHES, :], c_in[k][:, 0:D], scale[k % 2][0:PATCHES, TPB:TPB + 1],
                                             gain_ctx[:], ALU.mult, ALU.mult).then_inc(patch_ready, 1)

                def onehots(row, k):
                    wait_count(eng, mixed, TPB * (row - 1))
                    eng.tensor_scalar(onehot[k % 2][0:PATCHES, :], p_in[k][:], 1.0, rank[:], ALU.max, ALU.is_equal).then_inc(onehot_ready, 1)

                def lo_pool(row, k):
                    eng.wait_ge(pool_hi_ready, row + 1)
                    eng.tensor_tensor(pool_lo[k % 2][:], ps_d[0:ROWS, :], pool_hi[k % 2][:].bitcast(F32), ALU.subtract).then_inc(pool_lo_ready, 1)

                def lo_tile(n, j):
                    eng.wait_ge(hi_ready, n + 1)
                    eng.tensor_tensor(xt_lo[j][:], ps_t[j][:], xt_hi[j][:].bitcast(F32), ALU.subtract).then_inc(lo_ready, 1)

                def add_tile(n, row, k, t):
                    if t == 0:
                        wait_count(eng, x1_stored[k % 2], DMA * stores_before(row, k))
                    eng.wait_ge(mixed, n + 1)
                    eng.scalar_tensor_tensor(x1[k % 2][:, t, :], ps_o[t % 2][:], gate[:], x_in[k][:, t, :],
                                             ALU.mult, ALU.add).then_inc(x1_ready, 1)

                def stores_before(g, k):
                    return (GROUP // 2) * g + k // 2

                stats(0, 1, 0, range(TPB))
                spreads(0, 0)
                shifts(0, 0)
                patches(0, 0)
                onehots(0, 0)
                lo_pool(0, 0)
                lo_tile(0, 0)
                eng.wait_ge(gate_ready, 1)

                def turn(g, last=False):
                    for k in range(GROUP):
                        b = GROUP * g + k
                        nk = (k + 1) % GROUP
                        end = last and k == GROUP - 1
                        for t in range(TPB):
                            n = TPB * b + t
                            if not (end and t == TPB - 1):
                                lo_tile(n + 1, (t + 1) % 2)
                            if not end:
                                if t == 0:
                                    stats(b + 1, g + 1 + (k + 1) // GROUP, nk, (0, 1))
                                elif t == 1:
                                    stats(b + 1, g + 1 + (k + 1) // GROUP, nk, (2, 3))
                                    spreads(b + 1, nk)
                                elif t == 2:
                                    shifts(b + 1, nk)
                                    patches(b + 1, nk)
                                else:
                                    onehots(b + 1, nk)
                                    lo_pool(b + 1, nk)
                            add_tile(n, g, k, t)

                turn(0)
                with eng.Fori(1, LAST) as g:
                    turn(g)
                turn(LAST, last=True)


def route(nc, io, x1_dram, tokens_dram, table_dram):
    TURNS = TOKENS // (RT * P)
    x1_rows = x1_dram.rearrange("(g r) (t p) d -> g p (r t) d", r=RT // TPB, p=P)
    with ExitStack() as ctx:
        def sb(name, shape, dt=F32):
            return ctx.enter_context(nc.sbuf_tensor(name, shape, dt))

        def ps(name, shape):
            return ctx.enter_context(nc.psum_tensor(name, shape, F32))

        def sem(name):
            return ctx.enter_context(nc.semaphore(name))

        eye = sb("r_eye", [P, P])
        before = sb("before", [P, P], F16)
        all_ones = sb("all_ones", [P, P], F16)
        expert_id = sb("expert_id", [P, EXPERTS])
        half = sb("r_half", [P, RT])
        router_w = sb("router_w", [P, KC, EXPERTS])
        router_b = sb("router_b", [P, EXPERTS])
        gate_in = sb("r_gate_in", [P, 1])
        gate = sb("r_gate", [P, 1])
        fill = sb("fill", [P, EXPERTS * ET * 2], I32)
        token = sb("token", [P, RT])

        xs = sb("xs", [P, RT, D])
        xn = sb("r_xn", [P, RT, D])
        xt = [sb(f"r_xt{i}", [P, D]) for i in range(2)]
        tile_stats = sb("r_tile_stats", [P, RT, 6])
        moments = sb("r_moments", [P, RT, 2])
        spread = sb("r_spread", [P, RT])
        scale = sb("r_scale", [P, RT])
        logits = sb("logits", [P, RT, EXPERTS])
        top = sb("top", [P, RT, 8])
        top_at = sb("top_at", [P, RT, 8], U32)
        gap = sb("gap", [P, RT])
        second = sb("second", [P, RT])
        total = sb("total", [P, RT])
        weight = sb("weight", [P, TOP_K, RT])
        choice = sb("choice", [P, TOP_K, RT])
        chosen = sb("chosen", [P, TOP_K, RT, EXPERTS])
        either = sb("either", [P, RT, EXPERTS], F16)
        taken = sb("taken", [P, RT + 1, EXPERTS])
        place = sb("place", [P, RT, EXPERTS])
        picked = sb("picked", [P, TOP_K, RT, EXPERTS])
        own_place = sb("own_place", [P, TOP_K, RT])
        past = sb("past", [P, TOP_K, RT])
        slot_f = sb("slot_f", [P, TOP_K, RT])
        slot = sb("slot", [P, TOP_K * RT], I32)
        entry = sb("entry", [P, TOP_K * RT, 2], I32)
        least = sb("least", [P, 1])
        active = sb("active", [P, 1], I32)

        ps_t = [ps(f"r_ps_t{i}", [P, D]) for i in range(2)]
        ps_l = ps("ps_l", [P, RT * EXPERTS])
        ps_p = ps("ps_p", [P, 2, RT * EXPERTS])

        const_loaded = sem("r_const_loaded")
        xs_loaded = sem("xs_loaded")
        filled = sem("filled")
        entered = sem("entered")
        own = sem("r_own")
        step = sem("r_step")
        gate_ready = sem("r_gate_ready")
        gate_exp = sem("gate_exp")
        spread_ready = sem("r_spread_ready")
        scale_ready = sem("r_scale_ready")
        normed = sem("r_normed")
        turned = sem("r_turned")
        copied = sem("r_copied")
        scored = sem("scored")
        gap_ready = sem("gap_ready")
        either_ready = sem("either_ready")
        counted = sem("counted")
        entry_ready = sem("entry_ready")
        flag_ready = sem("flag_ready")
        passed = sem("passed_route")

        LOADS = [
            (eye, io["c_eye"]), (before, io["c_before"]), (expert_id, io["c_expert"]), (token, io["c_token"]),
            (router_w, io["router_w"].rearrange("(c p) e -> p c e", p=P)),
            (router_b, io["router_b"].partition_broadcast(P)), (gate_in, io["g_ffn"].partition_broadcast(P)),
            (fill, io["c_fill"]),
        ]

        def each_turn(eng, body):
            eng.wait_ge(flag_ready, 1)
            with eng.Fori(0, TURNS) as g:
                flag = eng.value_load(active[0:1, 0:1], min_val=0, max_val=1)
                with eng.If(flag > 0):
                    body(g)
                    hold(eng, flag_ready, g + 2, passed)

        with nc.Block() as block:

            @block.sync
            def _(eng):
                for dst, src in LOADS:
                    eng.dma_start(dst[:], src).then_inc(const_loaded, DMA)
                eng.wait_ge(const_loaded, DMA * len(LOADS))
                eng.dma_start(table_dram.rearrange("(p s) w -> p (s w)", p=P), fill[:]).then_inc(filled, DMA)
                eng.wait_ge(filled, DMA)

                def body(g):
                    eng.dma_start(xs[:], x1_rows[g]).then_inc(xs_loaded, DMA)
                each_turn(eng, body)

            @block.gpsimd
            def _(eng):
                eng.wait_ge(filled, DMA)

                def body(g):
                    eng.wait_ge(spread_ready, g + 1)
                    eng.tensor_tensor(scale[:], spread[:], half[:], ALU.pow).then_inc(scale_ready, 1)
                    hold(eng, entry_ready, g + 1, passed)
                    for s in range(TOP_K * RT):
                        eng.indirect_dma_start(
                            table_dram, bass.IndirectOffsetOnAxis(slot[:, s:s + 1], 0), entry[:, s, :], None,
                            bounds_check=EXPERTS * CAPACITY - 1, oob_is_err=False).then_inc(entered, DMA)
                        eng.indirect_dma_start(
                            tokens_dram, bass.IndirectOffsetOnAxis(slot[:, s:s + 1], 0), xn[:, s % RT, :], None,
                            bounds_check=EXPERTS * CAPACITY - 1, oob_is_err=False).then_inc(entered, DMA)
                    hold(eng, entered, 2 * DMA * TOP_K * RT * (g + 1), passed)

                each_turn(eng, body)

            @block.tensor
            def _(eng):
                def body(g):
                    for t in range(RT + 1):
                        if t < RT:
                            eng.wait_ge(normed, RT * g + t + 1)
                            if t >= 2:
                                eng.wait_ge(copied, RT * g + t - 1)
                            for c in range(KC):
                                mm = eng.transpose(ps_t[t % 2][:, c * P:(c + 1) * P], xn[:, t, c * P:(c + 1) * P], eye[:])
                            mm.then_inc(turned, 1)
                        if t > 0:
                            s = t - 1
                            eng.wait_ge(copied, RT * g + s + 1)
                            for c in range(KC):
                                mm = eng.matmul(ps_l[:, s * EXPERTS:(s + 1) * EXPERTS], xt[s % 2][:, c * P:(c + 1) * P],
                                                router_w[:, c, :], start=c == 0, stop=c == KC - 1)
                            mm.then_inc(scored, 1)
                    eng.wait_ge(either_ready, g + 1)
                    rhs = either[:].rearrange("p t e -> p (t e)")
                    eng.matmul(ps_p[:, 0, :], before[:], rhs, start=True, stop=True)
                    eng.matmul(ps_p[:, 1, :], all_ones[:], rhs, start=True, stop=True).then_inc(counted, 1)

                each_turn(eng, body)

            @block.scalar
            def _(eng):
                eng.wait_ge(const_loaded, DMA * len(LOADS))
                eng.activation(gate[:], gate_in[:], ACT.Tanh).then_inc(gate_ready, 1)

                def body(g):
                    for t in range(RT):
                        eng.wait_ge(turned, RT * g + t + 1)
                        if t >= 2:
                            eng.wait_ge(scored, RT * g + t - 1)
                        eng.activation(xt[t % 2][:], ps_t[t % 2][:], ACT.Copy).then_inc(copied, 1)
                    eng.wait_ge(gap_ready, g + 1)
                    eng.activation(second[:], gap[:], ACT.Exp).then_inc(gate_exp, 1)

                each_turn(eng, body)

            @block.vector
            def _(eng):
                eng.memset(half[:], -0.5)
                eng.memset(all_ones[:], 1.0)
                eng.memset(taken[:], 0.0)
                eng.memset(least[:], 1.0).then_inc(own, 1)
                eng.wait_ge(const_loaded, DMA * len(LOADS))
                eng.wait_ge(gate_ready, 1)
                eng.wait_ge(own, 1)
                eng.tensor_copy(active[:], least[:]).then_inc(flag_ready, 1)

                def body(g):
                    done = 0

                    def then(ins):
                        nonlocal done
                        done += 1
                        ins.then_inc(step, 1)

                    def own_steps():
                        hold(eng, step, STEPS * g + done, passed)

                    eng.wait_ge(xs_loaded, DMA * (g + 1))
                    for t in range(RT):
                        then(eng.bn_stats(tile_stats[:, t, :], xs[:, t, :]))
                    own_steps()
                    for t in range(RT):
                        then(eng.bn_aggr(moments[:, t, :], tile_stats[:, t, :]))
                    own_steps()
                    eng.tensor_scalar(spread[:], moments[:, :, 1], EPS, None, ALU.add).then_inc(spread_ready, 1)
                    eng.wait_ge(scale_ready, g + 1)
                    for t in range(RT):
                        eng.tensor_scalar(xn[:, t, :], xs[:, t, :], moments[:, t, 0:1], scale[:, t:t + 1],
                                          ALU.subtract, ALU.mult).then_inc(normed, 1)
                    eng.wait_ge(scored, RT * (g + 1))
                    then(eng.tensor_tensor(logits[:], ps_l[:].rearrange("p (t e) -> p t e", e=EXPERTS),
                                           router_b[:].unsqueeze(1).broadcast_to([P, RT, EXPERTS]), ALU.add))
                    own_steps()
                    for t in range(RT):
                        then(eng.max(top[:, t, :], logits[:, t, :]))
                    own_steps()
                    for t in range(RT):
                        then(eng.max_index(top_at[:, t, :], top[:, t, :], logits[:, t, :]))
                    eng.tensor_tensor(gap[:], top[:, :, 1], top[:, :, 0], ALU.subtract).then_inc(gap_ready, 1)
                    own_steps()
                    for k in range(TOP_K):
                        then(eng.tensor_copy(choice[:, k, :], top_at[:, :, k]))
                    own_steps()
                    for k in range(TOP_K):
                        then(eng.tensor_tensor(chosen[:, k], expert_id[:].unsqueeze(1).broadcast_to([P, RT, EXPERTS]),
                                               choice[:, k, :].unsqueeze(2).broadcast_to([P, RT, EXPERTS]), ALU.is_equal))
                    own_steps()
                    eng.tensor_tensor(either[:], chosen[:, 0], chosen[:, 1], ALU.add).then_inc(either_ready, 1)
                    eng.wait_ge(gate_exp, g + 1)
                    then(eng.tensor_scalar(total[:], second[:], 1.0, None, ALU.add))
                    own_steps()
                    then(eng.reciprocal(total[:], total[:]))
                    own_steps()
                    then(eng.tensor_scalar(weight[:, 0, :], total[:], gate[:], None, ALU.mult))
                    own_steps()
                    then(eng.tensor_tensor(weight[:, 1, :], weight[:, 0, :], second[:], ALU.mult))
                    eng.wait_ge(counted, g + 1)
                    for t in range(RT):
                        then(eng.tensor_tensor(taken[:, t + 1, :], taken[:, t, :], ps_p[:, 1, t * EXPERTS:(t + 1) * EXPERTS], ALU.add))
                        own_steps()
                    then(eng.tensor_tensor(place[:], ps_p[:, 0, :].rearrange("p (t e) -> p t e", e=EXPERTS), taken[:, 0:RT, :], ALU.add))
                    own_steps()
                    for k in range(TOP_K):
                        then(eng.tensor_tensor(picked[:, k], chosen[:, k], place[:], ALU.mult))
                    own_steps()
                    then(eng.tensor_reduce(own_place[:].rearrange("p k t -> p (k t)"), picked[:].rearrange("p k t e -> p (k t) e"), AX_X, ALU.add))
                    own_steps()
                    then(eng.tensor_scalar(past[:], own_place[:], float(CAPACITY), float(FAR), ALU.is_ge, ALU.mult))
                    then(eng.scalar_tensor_tensor(slot_f[:], choice[:], float(CAPACITY), own_place[:], ALU.mult, ALU.add))
                    own_steps()
                    then(eng.tensor_tensor(slot[:], slot_f[:].rearrange("p k t -> p (k t)"), past[:].rearrange("p k t -> p (k t)"), ALU.add))
                    for k in range(TOP_K):
                        then(eng.tensor_copy(entry[:, k * RT:(k + 1) * RT, 0], token[:]))
                    then(eng.tensor_copy(entry[:, :, 1].bitcast(F32), weight[:].rearrange("p k t -> p (k t)")))
                    own_steps()
                    eng.tensor_scalar(token[:], token[:], float(RT * P), None, ALU.add).then_inc(entry_ready, 1)
                    then(eng.tensor_copy(taken[:, 0, :], taken[:, RT, :]))
                    own_steps()
                    then(eng.tensor_reduce(least[:], taken[:, 0, :], AX_X, ALU.min))
                    own_steps()
                    eng.wait_ge(entered, 2 * DMA * TOP_K * RT * (g + 1))
                    eng.tensor_scalar(active[:], least[:], float(CAPACITY), None, ALU.is_lt).then_inc(flag_ready, 1)
                    steps_made.append(done)

                steps_made = []
                STEPS = 2 * RT + 1 + 2 * RT + 2 + 2 + 4 + RT + 1 + 2 + 1 + 2 + 1 + 2 + 1 + 2
                each_turn(eng, body)
                assert steps_made == [STEPS], (steps_made, STEPS)


def experts(nc, io, x1_dram, tokens_dram, table_dram):
    W_in, W_gate, W_out = io["W"], io["V"], io["W_out"]
    x1_rows = x1_dram.rearrange("b s d -> (b s) d")
    tok_rows = tokens_dram.rearrange("(e p t) d -> e p t d", e=EXPERTS, t=ET)
    QC = 2
    HALF = CAPACITY // 2
    with ExitStack() as ctx:
        def sb(name, shape, dt=F32):
            return ctx.enter_context(nc.sbuf_tensor(name, shape, dt))

        def ps(name, shape):
            return ctx.enter_context(nc.psum_tensor(name, shape, F32))

        def sem(name):
            return ctx.enter_context(nc.semaphore(name))

        eye = sb("e_eye", [P, P])
        lists = sb("lists", [P, EXPERTS, ET * 2], I32)
        this_ids = sb("this_ids", [P, ET], I32)
        this_w = sb("this_w", [P, ET])
        h_hi = sb("h_hi", [P, HC, CAPACITY], F32R)
        h_lo = sb("h_lo", [P, HC, CAPACITY], F32R)
        t_hi = sb("t_hi", [P, KC, CAPACITY], F32R)
        t_lo = sb("t_lo", [P, KC, CAPACITY], F32R)
        o_hi = sb("o_hi", [P, HC, D], F32R)
        o_lo = sb("o_lo", [P, HC, D], F32R)
        o_raw = [sb(f"o_raw{i}", [P, D]) for i in range(4)]
        wv_raw = [sb(f"wv_raw{i}", [P, 2, KC, QC * P]) for i in range(2)]
        wv_hi = [sb(f"wv_hi{i}", [P, 2, KC, P], F32R) for i in range(2)]
        wv_lo = [sb(f"wv_lo{i}", [P, 2, KC, P], F32R) for i in range(2)]
        silu = [sb(f"silu{i}", [P, HALF]) for i in range(2)]
        prod = [sb(f"prod{i}", [P, HALF]) for i in range(2)]
        tok = [sb(f"tok{i}", [P, D]) for i in range(4)]
        acc = [sb(f"acc{i}", [P, D]) for i in range(4)]
        new = [sb(f"new{i}", [P, D]) for i in range(2)]

        ps_g = [ps(f"ps_g{i}", [P, HALF]) for i in range(2)]
        ps_a = [ps(f"ps_a{i}", [P, HALF]) for i in range(2)]
        ps_y = [ps(f"ps_y{i}", [P, D]) for i in range(2)]
        ps_t = [ps(f"e_ps_t{i}", [P, D]) for i in range(2)]

        const_loaded = sem("e_const_loaded")
        cleared = sem("cleared")
        wv_loaded = [sem(f"wv_loaded{i}") for i in range(2)]
        o_loaded = [sem(f"o_loaded{i}") for i in range(4)]
        ids_ready = sem("ids_ready")
        weights_ready = sem("weights_ready")
        tok_loaded = [sem(f"tok_loaded{i}") for i in range(4)]
        acc_gathered = [sem(f"acc_gathered{i}") for i in range(4)]
        scattered = [sem(f"scattered{i}") for i in range(2)]
        wv_hi_ready = sem("wv_hi_ready")
        wv_lo_ready = sem("wv_lo_ready")
        o_hi_ready = sem("o_hi_ready")
        o_lo_ready = sem("o_lo_ready")
        gated = sem("gated")
        raised = sem("raised")
        silu_ready = sem("silu_ready")
        prod_ready = sem("prod_ready")
        h_hi_ready = sem("h_hi_ready")
        h_lo_ready = sem("h_lo_ready")
        turned = sem("e_turned")
        t_hi_ready = sem("t_hi_ready")
        t_lo_ready = sem("t_lo_ready")
        lowered = sem("lowered")
        new_ready = sem("new_ready")
        passed = sem("passed")

        def loop(eng, body):
            body(0, False)
            with eng.Fori(1, EXPERTS - 1) as e:
                body(e, False)
            body(EXPERTS - 1, True)

        with nc.Block() as block:

            @block.sync
            def _(eng):
                eng.dma_start(eye[:], io["c_eye"]).then_inc(const_loaded, DMA)
                eng.dma_start(lists[:], table_dram.rearrange("(e p t) w -> p e (t w)", p=P, t=ET)).then_inc(const_loaded, DMA)

                def load_tile(e, t):
                    wait_count(eng, turned, ET * e + t - 3)
                    eng.dma_start(tok[t % 4][:], tok_rows[e][:, t, :]).then_inc(tok_loaded[t % 4], DMA)

                def load_weights(e, q):
                    i = q % 2
                    quarter = HC // QC * e + q
                    wait_count(eng, wv_hi_ready, QC * (quarter - 1))
                    wait_count(eng, wv_lo_ready, QC * (quarter - 1))
                    for m, w in enumerate((W_in, W_gate)):
                        src = w[e][:, q * QC * P:(q + 1) * QC * P].rearrange("(c p) h -> p c h", p=P)
                        eng.dma_start(wv_raw[i][:, m], src).then_inc(wv_loaded[i], DMA)
                    for h in range(QC * q, QC * (q + 1)):
                        wait_count(eng, o_hi_ready, HC * e + h - 3)
                        wait_count(eng, o_lo_ready, HC * e + h - 3)
                        eng.dma_start(o_raw[h % 4][:], W_out[e][h * P:(h + 1) * P, :]).then_inc(o_loaded[h % 4], DMA)

                load_weights(0, 0)
                for t in range(ET):
                    load_tile(0, t)

                def body(e, last):
                    for q in range(1, HC // QC):
                        load_weights(e, q)
                    if not last:
                        load_weights(e + 1, 0)
                        for t in range(ET):
                            load_tile(e + 1, t)

                loop(eng, body)

            @block.gpsimd
            def _(eng):
                bound = dict(bounds_check=TOKENS - 1, oob_is_err=False)

                def gather_acc(n, t, first):
                    if not first:
                        hold(eng, new_ready, n - 3, passed)
                    eng.indirect_dma_start(acc[t % 4][:], None, x1_rows, bass.IndirectOffsetOnAxis(this_ids[:, t:t + 1], 0),
                                           **bound).then_inc(acc_gathered[t % 4], DMA)

                def scatter(n, t):
                    hold(eng, new_ready, n + 1, passed)
                    eng.indirect_dma_start(x1_rows, bass.IndirectOffsetOnAxis(this_ids[:, t:t + 1], 0), new[t % 2][:], None,
                                           **bound).then_inc(scattered[t % 2], DMA)

                eng.wait_ge(const_loaded, 2 * DMA)
                eng.wait_ge(cleared, 1)

                def body(e, last):
                    own = lists[:, bass.ds(e, 1), :].rearrange("p o (t w) -> p (o t) w", w=2)[:, :, 0]
                    for i in range(2):
                        if not isinstance(e, int) or e > 0:
                            hold(eng, scattered[i], DMA * (ET // 2) * e, passed)
                    eng.tensor_copy(this_ids[:], own).then_inc(ids_ready, 1)
                    hold(eng, ids_ready, e + 1, passed)
                    for t in range(4):
                        gather_acc(ET * e + t, t, isinstance(e, int) and e == 0)
                    for t in range(ET):
                        scatter(ET * e + t, t)
                        if t + 4 < ET:
                            gather_acc(ET * e + t + 4, t + 4, False)

                loop(eng, body)
                for i in range(2):
                    eng.wait_ge(scattered[i], DMA * (ET // 2) * EXPERTS)

            @block.tensor
            def _(eng):
                def turn_tile(n, turn_no, t):
                    eng.wait_ge(tok_loaded[t % 4], DMA * (2 * turn_no + t // 4 + 1))
                    wait_count(eng, t_hi_ready, n - 1)
                    wait_count(eng, t_lo_ready, n - 1)
                    for c in range(KC):
                        mm = eng.transpose(ps_t[t % 2][:, c * P:(c + 1) * P], tok[t % 4][:, c * P:(c + 1) * P], eye[:])
                    mm.then_inc(turned, 1)

                def product(out, stationary, moving, i, first, last):
                    (s_hi, s_lo), (m_hi, m_lo) = stationary, moving
                    eng.matmul(out, s_hi, m_hi, start=first, stop=False)
                    eng.matmul(out, s_hi, m_lo, start=False, stop=False)
                    return eng.matmul(out, s_lo, m_hi, start=False, stop=last)

                def raise_half(out, m, i, half):
                    cols = slice(half * HALF, (half + 1) * HALF)
                    for c in range(KC):
                        mm = product(out, (wv_hi[i][:, m, c, :], wv_lo[i][:, m, c, :]),
                                     (t_hi[:, c, cols], t_lo[:, c, cols]), c, c == 0, c == KC - 1)
                    return mm

                eng.wait_ge(const_loaded, 2 * DMA)
                for t in range(ET):
                    turn_tile(t, 0, t)

                def body(e, last):
                    eng.wait_ge(t_hi_ready, ET * (e + 1))
                    eng.wait_ge(t_lo_ready, ET * (e + 1))
                    for h in range(HC):
                        chunk = HC * e + h
                        eng.wait_ge(wv_hi_ready, chunk + 1)
                        eng.wait_ge(wv_lo_ready, chunk + 1)
                        for s in range(2):
                            wait_count(eng, silu_ready, 2 * chunk + s - 1)
                            raise_half(ps_g[s][:], 1, h % 2, s).then_inc(gated, 1)
                            wait_count(eng, prod_ready, 2 * chunk + s - 1)
                            raise_half(ps_a[s][:], 0, h % 2, s).then_inc(raised, 1)
                    for t in range(ET):
                        if not last:
                            turn_tile(ET * (e + 1) + t, e + 1, t)
                        wait_count(eng, new_ready, ET * e + t - 1)
                        rows = slice(t * P, (t + 1) * P)
                        for h in range(HC):
                            if t == 0:
                                eng.wait_ge(h_hi_ready, 2 * (HC * e + h) + 1)
                                eng.wait_ge(h_lo_ready, 2 * (HC * e + h) + 1)
                                eng.wait_ge(o_hi_ready, HC * e + h + 1)
                                eng.wait_ge(o_lo_ready, HC * e + h + 1)
                            if t == ET // 2 and h == 0:
                                eng.wait_ge(h_hi_ready, 2 * HC * (e + 1))
                                eng.wait_ge(h_lo_ready, 2 * HC * (e + 1))
                            mm = product(ps_y[t % 2][:], (h_hi[:, h, rows], h_lo[:, h, rows]),
                                         (o_hi[:, h, :], o_lo[:, h, :]), h, h == 0, h == HC - 1)
                        mm.then_inc(lowered, 1)

                loop(eng, body)

            @block.scalar
            def _(eng):
                def split_wv(chunk, quarter_turn, h):
                    q = h // QC
                    eng.wait_ge(wv_loaded[q % 2], 2 * DMA * (2 * quarter_turn + q // 2 + 1))
                    wait_count(eng, raised, 2 * (chunk - 1))
                    cols = slice(h % QC * P, (h % QC + 1) * P)
                    eng.activation(wv_hi[h % 2][:].rearrange("p m c h -> p (m c) h"), wv_raw[q % 2][:, :, :, cols].rearrange("p m c h -> p (m c) h"),
                                   ACT.Copy).then_inc(wv_hi_ready, 1)

                def split_list_tile(e, t):
                    eng.wait_ge(turned, ET * e + t + 1)
                    if t == 0:
                        wait_count(eng, raised, 2 * HC * e)
                    eng.activation(t_hi[:, :, t * P:(t + 1) * P], ps_t[t % 2][:].rearrange("p (c s) -> p c s", c=KC),
                                   ACT.Copy).then_inc(t_hi_ready, 1)

                split_wv(0, 0, 0)
                for t in range(ET):
                    split_list_tile(0, t)

                def body(e, last):
                    for h in range(HC):
                        chunk = HC * e + h
                        if h + 1 < HC:
                            split_wv(chunk + 1, e, h + 1)
                        elif not last:
                            split_wv(chunk + 1, e + 1, 0)
                        eng.wait_ge(o_loaded[h % 4], DMA * (2 * e + h // 4 + 1))
                        if h == 0:
                            wait_count(eng, lowered, ET * e)
                        eng.activation(o_hi[:, h, :], o_raw[h % 4][:], ACT.Copy).then_inc(o_hi_ready, 1)
                        for s in range(2):
                            eng.wait_ge(gated, 2 * chunk + s + 1)
                            wait_count(eng, prod_ready, 2 * chunk + s - 1)
                            eng.activation(silu[s][:], ps_g[s][:], ACT.Silu).then_inc(silu_ready, 1)
                            eng.wait_ge(prod_ready, 2 * chunk + s + 1)
                            eng.activation(h_hi[:, h, s * HALF:(s + 1) * HALF], prod[s][:], ACT.Copy).then_inc(h_hi_ready, 1)
                    if not last:
                        for t in range(ET):
                            split_list_tile(e + 1, t)

                loop(eng, body)

            @block.vector
            def _(eng):
                for i in range(3):
                    eng.memset(acc[i][:], 0.0)
                eng.memset(acc[3][:], 0.0).then_inc(cleared, 1)
                eng.wait_ge(const_loaded, 2 * DMA)

                def split_wv(chunk, h):
                    q = h // QC
                    eng.wait_ge(wv_hi_ready, chunk + 1)
                    cols = slice(h % QC * P, (h % QC + 1) * P)
                    eng.tensor_tensor(wv_lo[h % 2][:].rearrange("p m c h -> p (m c) h"), wv_raw[q % 2][:, :, :, cols].rearrange("p m c h -> p (m c) h"),
                                      wv_hi[h % 2][:].bitcast(F32).rearrange("p m c h -> p (m c) h"), ALU.subtract).then_inc(wv_lo_ready, 1)

                def split_list_tile(e, t):
                    cols = slice(t * P, (t + 1) * P)
                    eng.wait_ge(t_hi_ready, ET * e + t + 1)
                    eng.tensor_tensor(t_lo[:, :, cols], ps_t[t % 2][:].rearrange("p (c s) -> p c s", c=KC),
                                      t_hi[:, :, cols].bitcast(F32), ALU.subtract).then_inc(t_lo_ready, 1)

                split_wv(0, 0)
                for t in range(ET):
                    split_list_tile(0, t)

                def body(e, last):
                    own_w = lists[:, bass.ds(e, 1), :].rearrange("p o (t w) -> p (o t) w", w=2)[:, :, 1].bitcast(F32)
                    if not isinstance(e, int) or e > 0:
                        hold(eng, new_ready, ET * e, passed)
                    eng.tensor_copy(this_w[:], own_w).then_inc(weights_ready, 1)
                    for h in range(HC):
                        chunk = HC * e + h
                        if h + 1 < HC:
                            split_wv(chunk + 1, h + 1)
                        elif not last:
                            split_wv(chunk + 1, 0)
                        eng.wait_ge(o_hi_ready, chunk + 1)
                        eng.tensor_tensor(o_lo[:, h, :], o_raw[h % 4][:], o_hi[:, h, :].bitcast(F32), ALU.subtract).then_inc(o_lo_ready, 1)
                        for s in range(2):
                            cols = slice(s * HALF, (s + 1) * HALF)
                            eng.wait_ge(silu_ready, 2 * chunk + s + 1)
                            eng.wait_ge(raised, 2 * chunk + s + 1)
                            wait_count(eng, h_hi_ready, 2 * chunk + s - 1)
                            eng.tensor_tensor(prod[s][:], ps_a[s][:], silu[s][:], ALU.mult).then_inc(prod_ready, 1)
                            eng.wait_ge(h_hi_ready, 2 * chunk + s + 1)
                            eng.tensor_tensor(h_lo[:, h, cols], prod[s][:], h_hi[:, h, cols].bitcast(F32), ALU.subtract).then_inc(h_lo_ready, 1)
                    eng.wait_ge(weights_ready, e + 1)
                    for t in range(ET):
                        if not last:
                            split_list_tile(e + 1, t)
                        eng.wait_ge(acc_gathered[t % 4], DMA * (2 * e + t // 4 + 1))
                        wait_count(eng, scattered[t % 2], DMA * (ET // 2 * e + t // 2))
                        eng.wait_ge(lowered, ET * e + t + 1)
                        eng.scalar_tensor_tensor(new[t % 2][:], ps_y[t % 2][:], this_w[:, t:t + 1], acc[t % 4][:],
                                                 ALU.mult, ALU.add).then_inc(new_ready, 1)

                loop(eng, body)


def kernel(**inputs):
    from concourse import bacc
    from concourse.bass_utils import run_bass_kernel_spmd

    x = np.asarray(inputs["x"])
    laid_out = {
        "x": x,
        "ctx": np.asarray(inputs["ctx_2048"]),
        "lens": np.asarray(inputs["mask_BxS2_if0"]).T,
        "g_xattn": np.asarray(inputs["g_xattn"]),
        "g_ffn": np.asarray(inputs["g_ffn"]),
        "w_in": np.asarray(inputs["L0_xattn_W_in"]).T,
        "b_in": np.asarray(inputs["L0_xattn_b_in"]).reshape(1, D),
        "gain_res": np.asarray(inputs["L0_xattn_g_res"]).reshape(KC, P).T,
        "gain_ctx": np.asarray(inputs["L0_xattn_g_init"]),
        "router_w": np.asarray(inputs["L0_ffn_router_w"]).T,
        "router_b": np.asarray(inputs["L0_ffn_router_b"]),
        "W": np.asarray(inputs["L0_ffn_W"]),
        "V": np.asarray(inputs["L0_ffn_V"]),
        "W_out": np.asarray(inputs["L0_ffn_W_out"]),
        **constants(),
    }
    nc = bacc.Bacc("TRN2", target_bir_lowering=False, num_devices=1)
    arrays, io = {}, {}
    for name, a in laid_out.items():
        arrays[f"in_{name}"] = np.ascontiguousarray(a)
        io[name] = nc.dram_tensor(f"in_{name}", a.shape, mybir.dt.from_np(a.dtype), kind="ExternalInput").ap()
    out = nc.dram_tensor("out_x", [BATCH, SEQ, D], F32, kind="ExternalOutput").ap()
    build(nc, io, out)
    result = run_bass_kernel_spmd(nc, [arrays], core_ids=[0])
    return result.results[0]["out_x"]


def build(nc, io, out):
    tokens_dram = nc.dram_tensor("tokens_dram", [EXPERTS * CAPACITY, D], F32, kind="Internal").ap()
    table_dram = nc.dram_tensor("table_dram", [EXPERTS * CAPACITY, 2], I32, kind="Internal").ap()
    mix(nc, io, out, tokens_dram)
    route(nc, io, out, tokens_dram, table_dram)
    experts(nc, io, out, tokens_dram, table_dram)
```

```python
from contextlib import ExitStack

import numpy as np
import concourse.bass as bass
from concourse import mybir

F32 = mybir.dt.float32
F32R = mybir.dt.float32r
F16 = mybir.dt.float16
I32 = mybir.dt.int32
U32 = mybir.dt.uint32
ALU = mybir.AluOpType
ACT = mybir.ActivationFunctionType
AX_X = mybir.AxisListType.X

P = 128
BATCH, SEQ, D = 64, 512, 512
TOKENS = BATCH * SEQ
PATCHES, D_CTX = 77, 1024
HIDDEN, EXPERTS, TOP_K = 1024, 8, 2
CAPACITY = 2 * 2048 * TOP_K // EXPERTS
EPS = 1e-5
KC = D // P
TPB = SEQ // P
HC = HIDDEN // P
ET = CAPACITY // P
ROWS = PATCHES + 1
GROUP = 4
META = 8
TOKEN, WEIGHT, CHOICE = D, D + 1, D + 3
ROW = D + META
FAR = 32768
DMA = 16

_LOGP = np.float32(-0.001)
_DT = -np.log(-np.expm1(_LOGP.astype(np.float64)))


def wait_count(eng, sem, count):
    if not isinstance(count, int) or count > 0:
        eng.wait_ge(sem, count)


def hold(eng, sem, count, passed):
    eng.wait_ge(sem, count)
    eng.sem_inc(passed)


def constants():
    decay = np.zeros((ROWS, ROWS))
    q, p = np.meshgrid(np.arange(PATCHES), np.arange(PATCHES))
    decay[:PATCHES, :PATCHES] = np.where(q >= p, np.exp(_LOGP) * np.exp(-_DT * np.maximum(q - p, 0)), 0.0)
    decay[PATCHES, PATCHES] = 1.0
    at = np.arange(P)
    carry = np.zeros((P, P), np.float32)
    carry[at[:BATCH], at[:BATCH] + BATCH] = 1.0
    blank = np.zeros((P, ROW), np.int32)
    blank[:, TOKEN] = TOKENS
    return {
        "c_eye": np.eye(P, dtype=np.float32),
        "c_decay": decay.astype(np.float32),
        "c_rank": np.arange(1, PATCHES + 1, dtype=np.float32)[:, None],
        "c_pos": (np.arange(SEQ // 2)[None, :] + np.where(at < BATCH, 0, SEQ // 2)[:, None]).astype(np.float16),
        "c_carry": carry,
        "c_before": (at[:, None] < at[None, :]).astype(np.float16),
        "c_expert": np.broadcast_to(np.arange(EXPERTS, dtype=np.float32), (P, EXPERTS)),
        "c_token": (np.arange(TPB)[None, :] * P + at[:, None]).astype(np.float32),
        "c_blank": blank.view(np.float32),
        "c_list_expert": np.broadcast_to(np.repeat(np.arange(EXPERTS, dtype=np.float32), ET), (P, EXPERTS * ET)),
    }


def mix(nc, io, x1_dram, tokens_dram):
    with ExitStack() as ctx:
        def sb(name, shape, dt=F32):
            return ctx.enter_context(nc.sbuf_tensor(name, shape, dt))

        def ps(name, shape):
            return ctx.enter_context(nc.psum_tensor(name, shape, F32))

        def sem(name):
            return ctx.enter_context(nc.semaphore(name))

        eye = sb("eye", [P, P])
        decay = sb("decay", [ROWS, ROWS])
        lens_i = sb("lens_i", [P, PATCHES], I32)
        lens = sb("lens", [P, PATCHES])
        nothing = sb("nothing", [P, PATCHES])
        ends = sb("ends", [P, ROWS])
        wraps = sb("wraps", [P, PATCHES])
        pos = sb("pos", [P, SEQ // 2], F16)
        marks = [sb(f"marks{i}", [P, SEQ // 2], F16) for i in range(2)]
        carry = sb("carry", [P, P])
        ended = sb("ended", [P, SEQ // 2])
        plug = sb("plug", [P, SEQ // 2], F16)
        rank = sb("rank", [PATCHES, 1])
        gate_in = sb("gate_in", [P, 1])
        gate = sb("gate", [P, 1])
        gain_res = sb("gain_res", [P, KC])
        gain_ctx = sb("gain_ctx", [PATCHES, D])
        half = sb("half", [P, 5])
        blank = sb("blank", [P, ROW])
        w_raw = sb("w_raw", [P, KC, D])
        w_hi = sb("w_hi", [P, KC, D], F32R)
        w_lo = sb("w_lo", [P, KC, D], F32R)
        x_in = [sb(f"x_in{i}", [P, TPB, D]) for i in range(GROUP)]
        c_in = [sb(f"c_in{i}", [PATCHES, D_CTX]) for i in range(GROUP)]
        p_in = [sb(f"p_in{i}", [PATCHES, SEQ], F16) for i in range(GROUP)]
        x1 = [sb(f"x1_{i}", [P, TPB, D]) for i in range(GROUP)]
        tile_stats = [sb(f"tile_stats{i}", [P, TPB, 6]) for i in range(2)]
        moments = [sb(f"moments{i}", [P, TPB, 2]) for i in range(2)]
        spread = [sb(f"spread{i}", [P, 5]) for i in range(2)]
        scale = [sb(f"scale{i}", [P, 5]) for i in range(2)]
        shift = [sb(f"shift{i}", [P, TPB]) for i in range(2)]
        squares = sb("squares", [PATCHES, D_CTX])
        sumsq = [sb(f"sumsq{i}", [PATCHES, 1]) for i in range(2)]
        patch = [sb(f"patch{i}", [ROWS, D]) for i in range(2)]
        pool_hi = [sb(f"pool_hi{i}", [ROWS, D], F32R) for i in range(2)]
        pool_lo = [sb(f"pool_lo{i}", [ROWS, D], F32R) for i in range(2)]
        onehot = [sb(f"onehot{i}", [ROWS, SEQ], F32R) for i in range(2)]
        xn = [sb(f"xn{i}", [P, D]) for i in range(2)]
        xt_hi = [sb(f"xt_hi{i}", [P, D], F32R) for i in range(2)]
        xt_lo = [sb(f"xt_lo{i}", [P, D], F32R) for i in range(2)]

        before = sb("before", [P, P], F16)
        all_ones = sb("all_ones", [P, P], F16)
        expert_id = sb("expert_id", [P, EXPERTS])
        router_w = sb("router_w", [P, KC, EXPERTS])
        router_b = sb("router_b", [P, EXPERTS])
        ffn_gate_in = sb("ffn_gate_in", [P, 1])
        ffn_gate = sb("ffn_gate", [P, 1])
        token = sb("token", [P, TPB])
        rows = [sb(f"rows{i}", [P, TPB, ROW]) for i in range(GROUP)]
        r_stats = [sb(f"r_stats{i}", [P, TPB, 6]) for i in range(2)]
        r_moments = [sb(f"r_moments{i}", [P, TPB, 2]) for i in range(2)]
        r_spread = [sb(f"r_spread{i}", [P, TPB]) for i in range(2)]
        r_scale = [sb(f"r_scale{i}", [P, TPB]) for i in range(2)]
        r_shift = [sb(f"r_shift{i}", [P, TPB]) for i in range(2)]
        r_xt = [sb(f"r_xt{i}", [P, D]) for i in range(2)]
        logits = sb("logits", [P, TPB, EXPERTS])
        top = sb("top", [P, TPB, 8])
        top_at = sb("top_at", [P, TPB, 8], U32)
        gap = sb("gap", [P, TPB])
        second = sb("second", [P, TPB])
        total = sb("total", [P, TPB])
        choice = sb("choice", [P, TOP_K, TPB])
        chosen = sb("chosen", [P, TOP_K * TPB, EXPERTS])
        either = sb("either", [P, TPB * EXPERTS], F16)
        taken = sb("taken", [P, EXPERTS])
        place = sb("place", [P, TPB, EXPERTS])
        picked = sb("picked", [P, TOP_K * TPB, EXPERTS])
        own_place = sb("own_place", [P, TOP_K * TPB])
        past = sb("past", [P, TOP_K * TPB])
        slot_f = sb("slot_f", [P, TOP_K * TPB])
        slot = [sb(f"slot{i}", [P, TOP_K * TPB], I32) for i in range(GROUP)]
        least = sb("least", [P, 1])
        active = sb("active", [P, 1], I32)

        ps_t = [ps(f"ps_t{i}", [P, D]) for i in range(2)]
        ps_o = [ps(f"ps_o{i}", [P, D]) for i in range(2)]
        ps_d = ps("ps_d", [P, D])
        ps_r = ps("ps_r", [P, D])
        ps_s = ps("ps_s", [P, TPB * EXPERTS])
        ps_p = ps("ps_p", [P, (TPB + 1) * EXPERTS])
        ps_c = ps_r

        marks_loaded = sem("marks_loaded")
        const_loaded = sem("const_loaded")
        plug_stored = sem("plug_stored")
        tokens_cleared = sem("tokens_cleared")
        batch_loaded = [sem(f"batch_loaded{i}") for i in range(GROUP)]
        plug_loaded = [sem(f"plug_loaded{i}") for i in range(GROUP)]
        x1_stored = [sem(f"x1_stored{i}") for i in range(GROUP)]
        const_set = sem("const_set")
        prep = sem("prep")
        marked = sem("marked")
        ended_ready = sem("ended_ready")
        carried = sem("carried")
        plug_ready = sem("plug_ready")
        w_scaled = sem("w_scaled")
        w_hi_ready = sem("w_hi_ready")
        w_lo_ready = sem("w_lo_ready")
        gate_ready = sem("gate_ready")
        stats_done = sem("stats_done")
        moments_done = sem("moments_done")
        sumsq_ready = sem("sumsq_ready")
        spread_ready = sem("spread_ready")
        scale_ready = sem("scale_ready")
        shift_ready = sem("shift_ready")
        normed = sem("normed")
        turned = sem("turned")
        hi_ready = sem("hi_ready")
        lo_ready = sem("lo_ready")
        mixed = sem("mixed")
        x1_ready = sem("x1_ready")
        patch_ready = sem("patch_ready")
        pooled = sem("pooled")
        pool_hi_ready = sem("pool_hi_ready")
        pool_lo_ready = sem("pool_lo_ready")
        onehot_ready = sem("onehot_ready")
        passed = sem("passed_mix")
        r_stats_done = sem("r_stats_done")
        r_moments_done = sem("r_moments_done")
        r_spread_ready = sem("r_spread_ready")
        r_scale_ready = sem("r_scale_ready")
        r_shift_ready = sem("r_shift_ready")
        r_normed = sem("r_normed")
        r_turned = sem("r_turned")
        r_copied = sem("r_copied")
        scored = sem("scored")
        logits_ready = sem("logits_ready")
        gap_ready = sem("gap_ready")
        second_ready = sem("second_ready")
        either_ready = sem("either_ready")
        counted = sem("counted")
        taken_ready = sem("taken_ready")
        step = sem("step")
        routed = sem("routed")
        entered = [sem(f"entered{i}") for i in range(GROUP)]
        least_ready = sem("least_ready")
        flag_ready = sem("flag_ready")

        plug_dram = nc.dram_tensor("plug_dram", [BATCH, SEQ], F16, kind="Internal").ap()
        LOADS = [
            (w_raw, io["w_in"].rearrange("(c p) e -> p c e", p=P)), (gain_res, io["gain_res"]),
            (eye, io["c_eye"]), (decay, io["c_decay"]), (rank, io["c_rank"]), (carry, io["c_carry"]),
            (gain_ctx, io["gain_ctx"][0:D].partition_broadcast(PATCHES)),
            (gate_in, io["g_xattn"].partition_broadcast(P)), (blank, io["c_blank"]),
            (before, io["c_before"]), (expert_id, io["c_expert"]), (token, io["c_token"]),
            (router_w, io["router_w"].rearrange("(c p) e -> p c e", p=P)),
            (router_b, io["router_b"].partition_broadcast(P)), (ffn_gate_in, io["g_ffn"].partition_broadcast(P)),
        ]
        CONSTS = DMA * (len(LOADS) + 2)
        MARKS = 6
        FILLS = 4
        LAST = BATCH // GROUP - 1
        STEPS = (2 * TPB + 2) + 3 + 9

        def there(row):
            return not isinstance(row, int) or 0 <= row < BATCH

        def turns(eng, turn, after):
            turn(0, True, False)
            turn(1, True, False)

            def flagged(body, otherwise):
                flag = eng.value_load(active[0:1, 0:1], min_val=0, max_val=1)
                with eng.If(flag > 0):
                    body()
                with eng.Else():
                    otherwise()

            with eng.Fori(2, LAST) as g:
                flagged(lambda: turn(g, True, False), lambda: turn(g, False, False))
            flagged(lambda: turn(LAST, True, True), lambda: turn(LAST, False, True))
            flag = eng.value_load(active[0:1, 0:1], min_val=0, max_val=1)
            with eng.If(flag > 0):
                for b in range(BATCH, BATCH + 3):
                    after(b, b % GROUP)

        with nc.Block() as block:

            @block.sync
            def _(eng):
                def load(b, k):
                    eng.dma_start(x_in[k][:], io["x"][b].rearrange("(t p) d -> p t d", p=P)).then_inc(batch_loaded[k], DMA)
                    eng.dma_start(c_in[k][:], io["ctx"][b]).then_inc(batch_loaded[k], DMA)

                def load_plug(b, k):
                    eng.dma_start(p_in[k][:], plug_dram[b].partition_broadcast(PATCHES)).then_inc(plug_loaded[k], DMA)

                def fill(i):
                    part = tokens_dram.rearrange("(f n p) d -> f p n d", f=FILLS, p=P)[i]
                    eng.dma_start(part, blank[:].unsqueeze(1).broadcast_to([P, EXPERTS * ET // FILLS, ROW])).then_inc(tokens_cleared, DMA)

                halves = plug_dram.rearrange("b (h s) -> h b s", h=2)
                for h in range(2):
                    eng.dma_start(lens_i[h * BATCH:(h + 1) * BATCH, :], io["lens"]).then_inc(marks_loaded, DMA)
                eng.dma_start(pos[:], io["c_pos"]).then_inc(marks_loaded, DMA)
                load(0, 0)
                eng.wait_ge(const_set, 4)
                for i in range(2):
                    eng.dma_start(patch[i][PATCHES:ROWS, :], io["b_in"]).then_inc(const_loaded, DMA)
                for k in range(1, GROUP):
                    load(k, k)
                eng.wait_ge(const_loaded, CONSTS)
                fill(0)
                eng.wait_ge(plug_ready, 1)
                for h in range(2):
                    eng.dma_start(halves[h], plug[h * BATCH:(h + 1) * BATCH, :]).then_inc(plug_stored, DMA)
                eng.wait_ge(plug_stored, 2 * DMA)
                for k in range(GROUP):
                    load_plug(k, k)

                def turn(g, last=False, filling=False):
                    for k in range(GROUP):
                        b = GROUP * g + k
                        if filling and k + 1 < FILLS:
                            fill(k + 1)
                        eng.wait_ge(x1_ready, TPB * (b + 1))
                        eng.dma_start(x1_dram[b].rearrange("(t p) d -> p t d", p=P), x1[k][:]).then_inc(x1_stored[k], DMA)
                        if not last:
                            load(b + GROUP, k)
                            load_plug(b + GROUP, k)

                turn(0, filling=True)
                with eng.Fori(1, LAST) as g:
                    turn(g)
                turn(LAST, last=True)
                for i in range(GROUP):
                    eng.wait_ge(x1_stored[i], DMA * (BATCH // GROUP))

            @block.gpsimd
            def _(eng):
                def root(b, k):
                    eng.wait_ge(spread_ready, 2 * (b + 1))
                    wait_count(eng, normed, TPB * (b - 1))
                    eng.tensor_tensor(scale[k % 2][:], spread[k % 2][:], half[:], ALU.pow).then_inc(scale_ready, 1)

                def r_root(r, k):
                    eng.wait_ge(r_spread_ready, r + 1)
                    wait_count(eng, r_normed, TPB * (r - 1))
                    eng.tensor_tensor(r_scale[k % 2][:], r_spread[k % 2][:], half[:, 0:TPB], ALU.pow).then_inc(r_scale_ready, 1)

                def enter(r, k):
                    hold(eng, routed, r + 1, passed)
                    for s in range(TOP_K * TPB):
                        eng.indirect_dma_start(
                            tokens_dram, bass.IndirectOffsetOnAxis(slot[k][:, s:s + 1], 0), rows[k][:, s % TPB, :], None,
                            bounds_check=EXPERTS * CAPACITY - 1, oob_is_err=False).then_inc(entered[k], DMA)

                def route_roots(b, k):
                    if there(b - 1):
                        r_root(b - 1, (k - 1) % GROUP)

                def route_enter(b, k):
                    if there(b - 3):
                        enter(b - 3, (k - 3) % GROUP)

                eng.wait_ge(const_set, 4)
                for c in range(KC):
                    eng.wait_ge(w_hi_ready, c + 1)
                    eng.tensor_tensor(w_lo[:, c, :], w_raw[:, c, :], w_hi[:, c, :].bitcast(F32), ALU.subtract).then_inc(w_lo_ready, 1)
                root(0, 0)
                root(1, 1)

                def turn(g, routing, last):
                    for k in range(GROUP):
                        b = GROUP * g + k
                        if isinstance(b, int) and b == 3:
                            eng.wait_ge(tokens_cleared, FILLS * DMA)
                        if not (last and k >= GROUP - 2):
                            root(b + 2, (k + 2) % GROUP)
                        if routing:
                            route_roots(b, k)
                            route_enter(b, k)
                    if routing and not (isinstance(g, int) and g == 0):
                        hold(eng, flag_ready, g, passed)

                def after(b, k):
                    route_roots(b, k)
                    route_enter(b, k)

                turns(eng, turn, after)
                eng.drain()

            @block.tensor
            def _(eng):
                def turn_tile(n, j):
                    eng.wait_ge(normed, n + 1)
                    wait_count(eng, hi_ready, n - 1)
                    wait_count(eng, lo_ready, n - 1)
                    for c in range(KC):
                        mm = eng.transpose(ps_t[j][:, c * P:(c + 1) * P], xn[j][:, c * P:(c + 1) * P], eye[:])
                    mm.then_inc(turned, 1)

                def depool(b, k):
                    eng.wait_ge(patch_ready, b + 1)
                    wait_count(eng, pool_hi_ready, b)
                    wait_count(eng, pool_lo_ready, b)
                    eng.matmul(ps_d[0:ROWS, :], decay[:], patch[k % 2][:], start=True, stop=True).then_inc(pooled, 1)

                def mix_tile(n, b, k, t, between):
                    j = t % 2
                    eng.wait_ge(hi_ready, n + 1)
                    eng.wait_ge(lo_ready, n + 1)
                    wait_count(eng, x1_ready, n - 1)
                    for c in range(KC):
                        own = slice(c * P, (c + 1) * P)
                        eng.matmul(ps_o[j][:], xt_hi[j][:, own], w_hi[:, c, :], start=c == 0, stop=False)
                        eng.matmul(ps_o[j][:], xt_hi[j][:, own], w_lo[:, c, :], start=False, stop=False)
                        eng.matmul(ps_o[j][:], xt_lo[j][:, own], w_hi[:, c, :], start=False, stop=False)
                        if c == 1:
                            between()
                    if t == 0:
                        eng.wait_ge(onehot_ready, b + 1)
                        eng.wait_ge(pool_hi_ready, b + 1)
                        eng.wait_ge(pool_lo_ready, b + 1)
                    own = slice(t * P, (t + 1) * P)
                    eng.matmul(ps_o[j][:], onehot[k % 2][:, own], pool_hi[k % 2][:], start=False, stop=False)
                    eng.matmul(ps_o[j][:], onehot[k % 2][:, own], pool_lo[k % 2][:], start=False, stop=True).then_inc(mixed, 1)

                def route_step(b, k, t):
                    q, r = (t - 2) % TPB, (b - 3 if t < 2 else b - 2)
                    if there(r):
                        eng.wait_ge(r_copied, TPB * r + q + 1)
                        if q == 0:
                            wait_count(eng, logits_ready, r)
                        for c in range(KC):
                            mm = eng.matmul(ps_s[:, q * EXPERTS:(q + 1) * EXPERTS], r_xt[q % 2][:, c * P:(c + 1) * P],
                                            router_w[:, c, :], start=c == 0, stop=c == KC - 1)
                        mm.then_inc(scored, 1)
                    q, r = (t - 1) % TPB, (b - 3 if t < 1 else b - 2)
                    if there(r):
                        slot_k = (k - 3 if t < 1 else k - 2) % GROUP
                        eng.wait_ge(r_normed, TPB * r + q + 1)
                        wait_count(eng, r_copied, TPB * r + q)
                        for c in range(KC):
                            mm = eng.transpose(ps_r[:, c * P:(c + 1) * P], rows[slot_k][:, q, c * P:(c + 1) * P], eye[:])
                        mm.then_inc(r_turned, 1)
                    if t == 2 and there(b - 3):
                        eng.wait_ge(either_ready, b - 2)
                        wait_count(eng, taken_ready, b - 3)
                        eng.matmul(ps_p[:, 0:TPB * EXPERTS], before[:], either[:], start=True, stop=False, skip_group_check=True)
                        for d in range(1, TPB + 1):
                            mm = eng.matmul(ps_p[:, d * EXPERTS:], all_ones[:], either[:, 0:(TPB + 1 - d) * EXPERTS],
                                            start=False, stop=d == TPB, skip_group_check=True)
                        mm.then_inc(counted, 1)

                eng.wait_ge(const_loaded, CONSTS)
                depool(0, 0)
                turn_tile(0, 0)

                eng.wait_ge(ended_ready, 1)
                eng.matmul(ps_c[:, 0:1], carry[:], ended[:, SEQ // 2 - 1:], start=True, stop=True).then_inc(carried, 1)
                eng.wait_ge(w_hi_ready, KC)
                eng.wait_ge(w_lo_ready, KC)
                eng.wait_ge(plug_ready, 1)

                def turn(g, routing, last):
                    for k in range(GROUP):
                        b = GROUP * g + k
                        end = last and k == GROUP - 1
                        for t in range(TPB):
                            n = TPB * b + t
                            if not (end and t == TPB - 1):
                                turn_tile(n + 1, (t + 1) % 2)
                            if t == TPB - 1 and not end:
                                depool(b + 1, k + 1)
                            mix_tile(n, b, k, t, lambda: route_step(b, k, t) if routing else None)
                    if routing and not (isinstance(g, int) and g == 0):
                        hold(eng, flag_ready, g, passed)

                def after(b, k):
                    for t in range(TPB):
                        route_step(b, k, t)

                turns(eng, turn, after)

            @block.scalar
            def _(eng):
                for dst, src in LOADS:
                    eng.dma_start(dst[:], src).then_inc(const_loaded, DMA)

                def square_row(row, turn_no, k):
                    eng.wait_ge(batch_loaded[k], 2 * DMA * turn_no)
                    wait_count(eng, spread_ready, 2 * (row - 1))
                    wait_count(eng, sumsq_ready, row)
                    eng.activation(squares[:], c_in[k][:], ACT.Square, accum_out=sumsq[k % 2][:]).then_inc(sumsq_ready, 1)

                def norm_tile(n, row, k, t):
                    if t == 0:
                        eng.wait_ge(shift_ready, row + 1)
                    wait_count(eng, turned, n - 1)
                    eng.activation(xn[t % 2][:], x_in[k][:, t, :], ACT.Identity, bias=shift[k % 2][:, t:t + 1],
                                   scale=scale[k % 2][:, t:t + 1]).then_inc(normed, 1)

                def hi_tile(n, j):
                    eng.wait_ge(turned, n + 1)
                    wait_count(eng, mixed, n - 1)
                    eng.activation(xt_hi[j][:], ps_t[j][:], ACT.Copy).then_inc(hi_ready, 1)

                def hi_pool(row, k):
                    eng.wait_ge(pooled, row + 1)
                    wait_count(eng, mixed, TPB * (row - 1))
                    eng.activation(pool_hi[k % 2][:], ps_d[0:ROWS, :], ACT.Copy).then_inc(pool_hi_ready, 1)

                eng.wait_ge(const_loaded, CONSTS)
                eng.activation(gate[:], gate_in[:], ACT.Tanh).then_inc(gate_ready, 1)
                eng.activation(ffn_gate[:], ffn_gate_in[:], ACT.Tanh).then_inc(gate_ready, 1)
                for c in range(KC):
                    eng.activation(w_raw[:, c, :], w_raw[:, c, :], ACT.Copy, scale=gain_res[:, c:c + 1]).then_inc(w_scaled, 1)
                for c in range(KC):
                    eng.wait_ge(w_scaled, c + 1)
                    eng.activation(w_hi[:, c, :], w_raw[:, c, :], ACT.Copy).then_inc(w_hi_ready, 1)
                square_row(0, 1, 0)
                square_row(1, 1, 1)
                norm_tile(0, 0, 0, 0)
                norm_tile(1, 0, 0, 1)
                hi_pool(0, 0)
                hi_tile(0, 0)

                def route_step(g, b, k, t):
                    r = b - 2
                    if there(r):
                        slot_k = (k - 2) % GROUP
                        if t == 0:
                            eng.wait_ge(r_shift_ready, r + 1)
                            if not isinstance(r, int) or r >= GROUP:
                                eng.wait_ge(entered[slot_k], TOP_K * TPB * DMA * (g if k >= 2 else g - 1))
                        eng.activation(rows[slot_k][:, t, 0:D], x1[slot_k][:, t, :], ACT.Identity,
                                       bias=r_shift[k % 2][:, t:t + 1], scale=r_scale[k % 2][:, t:t + 1]).then_inc(r_normed, 1)
                    q, r = (t - 1) % TPB, (b - 3 if t < 1 else b - 2)
                    if there(r):
                        eng.wait_ge(r_turned, TPB * r + q + 1)
                        wait_count(eng, scored, TPB * r + q - 1)
                        eng.activation(r_xt[q % 2][:], ps_r[:], ACT.Copy).then_inc(r_copied, 1)
                    if t == 2 and there(b - 3):
                        eng.wait_ge(gap_ready, b - 2)
                        eng.activation(second[:], gap[:], ACT.Exp).then_inc(second_ready, 1)

                def turn(g, routing, last):
                    for k in range(GROUP):
                        b = GROUP * g + k
                        nk = (k + 1) % GROUP
                        end = last and k == GROUP - 1
                        for t in range(TPB):
                            n = TPB * b + t
                            if not (end and t == TPB - 1):
                                hi_tile(n + 1, (t + 1) % 2)
                            if t + 2 < TPB:
                                norm_tile(n + 2, b, k, t + 2)
                            elif not end:
                                norm_tile(n + 2, b + 1, nk, t + 2 - TPB)
                            if t == 0 and not (last and k >= GROUP - 2):
                                square_row(b + 2, g + 1 + (k + 2) // GROUP, (k + 2) % GROUP)
                            if t == TPB - 1 and not end:
                                hi_pool(b + 1, nk)
                            if routing:
                                route_step(g, b, k, t)
                    if routing and not (isinstance(g, int) and g == 0):
                        hold(eng, flag_ready, g, passed)

                def after(b, k):
                    for t in range(TPB):
                        route_step(b // GROUP, b, k, t)

                turns(eng, turn, after)

            @block.vector
            def _(eng):
                for i in range(2):
                    eng.memset(spread[i][:], 1.0)
                    eng.memset(onehot[i][:].bitcast(F32), 1.0).then_inc(const_set, 1)
                eng.memset(half[:], -0.5).then_inc(const_set, 1)
                for i in range(2):
                    eng.memset(marks[i][:], 0.0)
                eng.memset(nothing[:], 0.0)
                eng.memset(ends[:], -1e6)
                eng.memset(taken[:], 0.0)
                eng.memset(all_ones[:], 1.0)
                for i in range(GROUP):
                    eng.memset(rows[i][:, :, CHOICE + TOP_K:], 0.0)
                eng.memset(patch[0][:], 0.0)
                eng.memset(patch[1][:], 0.0).then_inc(const_set, 1)

                def stats(row, turn_no, k, tiles):
                    if tiles[0] == 0:
                        eng.wait_ge(batch_loaded[k], 2 * DMA * turn_no)
                    for t in tiles:
                        eng.bn_stats(tile_stats[k % 2][:, t, :], x_in[k][:, t, :]).then_inc(stats_done, 1)

                def spreads(row, k):
                    hold(eng, stats_done, TPB * (row + 1), passed)
                    for t in range(TPB):
                        eng.bn_aggr(moments[k % 2][:, t, :], tile_stats[k % 2][:, t, :]).then_inc(moments_done, 1)
                    eng.wait_ge(moments_done, TPB * (row + 1))
                    eng.tensor_scalar(spread[k % 2][:, 0:TPB], moments[k % 2][:, :, 1], 1.0 + EPS, EPS * EPS,
                                      ALU.mult, ALU.add).then_inc(spread_ready, 1)
                    eng.wait_ge(sumsq_ready, row + 1)
                    eng.tensor_scalar(spread[k % 2][0:PATCHES, TPB:TPB + 1], sumsq[k % 2][:], 1.0 / D_CTX, EPS,
                                      ALU.mult, ALU.add).then_inc(spread_ready, 1)

                def shifts(row, k):
                    eng.wait_ge(scale_ready, row + 1)
                    eng.scalar_tensor_tensor(shift[k % 2][:], moments[k % 2][:, :, 0], -1.0, scale[k % 2][:, 0:TPB],
                                             ALU.mult, ALU.mult).then_inc(shift_ready, 1)

                def patches(row, k):
                    wait_count(eng, pooled, row - 1)
                    eng.scalar_tensor_tensor(patch[k % 2][0:PATCHES, :], c_in[k][:, 0:D], scale[k % 2][0:PATCHES, TPB:TPB + 1],
                                             gain_ctx[:], ALU.mult, ALU.mult).then_inc(patch_ready, 1)

                def onehots(row, turn_no, k):
                    eng.wait_ge(plug_loaded[k], DMA * turn_no)
                    wait_count(eng, mixed, TPB * (row - 1))
                    eng.tensor_scalar(onehot[k % 2][0:PATCHES, :], p_in[k][:], 1.0, rank[:], ALU.max, ALU.is_equal).then_inc(onehot_ready, 1)

                def lo_pool(row, k):
                    eng.wait_ge(pool_hi_ready, row + 1)
                    eng.tensor_tensor(pool_lo[k % 2][:], ps_d[0:ROWS, :], pool_hi[k % 2][:].bitcast(F32), ALU.subtract).then_inc(pool_lo_ready, 1)

                def lo_tile(n, j):
                    eng.wait_ge(hi_ready, n + 1)
                    eng.tensor_tensor(xt_lo[j][:], ps_t[j][:], xt_hi[j][:].bitcast(F32), ALU.subtract).then_inc(lo_ready, 1)

                def add_tile(n, g, k, t):
                    if t == 0:
                        wait_count(eng, x1_stored[k], DMA * g)
                    eng.wait_ge(mixed, n + 1)
                    eng.scalar_tensor_tensor(x1[k][:, t, :], ps_o[t % 2][:], gate[:], x_in[k][:, t, :],
                                             ALU.mult, ALU.add).then_inc(x1_ready, 1)

                def r_stat(r, k, t):
                    eng.wait_ge(x1_ready, TPB * r + t + 1)
                    eng.bn_stats(r_stats[k % 2][:, t, :], x1[k][:, t, :]).then_inc(r_stats_done, 1)

                def r_spreads(r, k):
                    hold(eng, r_stats_done, TPB * (r + 1), passed)
                    for t in range(TPB):
                        eng.bn_aggr(r_moments[k % 2][:, t, :], r_stats[k % 2][:, t, :]).then_inc(r_moments_done, 1)
                    eng.wait_ge(r_moments_done, TPB * (r + 1))
                    eng.tensor_scalar(r_spread[k % 2][:], r_moments[k % 2][:, :, 1], EPS, None, ALU.add).then_inc(r_spread_ready, 1)

                def r_shifts(r, k):
                    eng.wait_ge(r_scale_ready, r + 1)
                    eng.scalar_tensor_tensor(r_shift[k % 2][:], r_moments[k % 2][:, :, 0], -1.0, r_scale[k % 2][:],
                                             ALU.mult, ALU.mult).then_inc(r_shift_ready, 1)

                class Steps:
                    done = 0

                    def then(self, ins):
                        self.done += 1
                        ins.then_inc(step, 1)

                    def settle(self, r):
                        hold(eng, step, STEPS * r + self.done, passed)

                own = Steps()
                spread_out = lambda ap: ap.unsqueeze(2).broadcast_to([P, TOP_K * TPB, EXPERTS])

                def choose(r, k):
                    own.done = 0
                    eng.wait_ge(scored, TPB * (r + 1))
                    eng.tensor_tensor(logits[:], ps_s[:].rearrange("p (t e) -> p t e", e=EXPERTS),
                                      router_b[:].unsqueeze(1).broadcast_to([P, TPB, EXPERTS]), ALU.add).then_inc(logits_ready, 1)
                    hold(eng, logits_ready, r + 1, passed)
                    for t in range(TPB):
                        own.then(eng.max(top[:, t, :], logits[:, t, :]))
                    own.settle(r)
                    for t in range(TPB):
                        own.then(eng.max_index(top_at[:, t, :], top[:, t, :], logits[:, t, :]))
                    eng.tensor_tensor(gap[:], top[:, :, 1], top[:, :, 0], ALU.subtract).then_inc(gap_ready, 1)
                    own.settle(r)
                    own.then(eng.tensor_copy(choice[:], top_at[:, :, 0:TOP_K].rearrange("p t k -> p k t")))
                    own.settle(r)
                    own.then(eng.tensor_tensor(chosen[:], expert_id[:].unsqueeze(1).broadcast_to([P, TOP_K * TPB, EXPERTS]),
                                               spread_out(choice[:].rearrange("p k t -> p (k t)")), ALU.is_equal))
                    own.settle(r)
                    eng.tensor_tensor(either[:], chosen[:, 0:TPB, :].rearrange("p t e -> p (t e)"),
                                      chosen[:, TPB:, :].rearrange("p t e -> p (t e)"), ALU.add).then_inc(either_ready, 1)

                def find_places(r, k):
                    eng.wait_ge(counted, r + 1)
                    own.then(eng.tensor_tensor(place[:], ps_p[:, 0:TPB * EXPERTS].rearrange("p (t e) -> p t e", e=EXPERTS),
                                               taken[:].unsqueeze(1).broadcast_to([P, TPB, EXPERTS]), ALU.add))
                    own.settle(r)
                    eng.tensor_tensor(taken[:], taken[:], ps_p[:, TPB * EXPERTS:], ALU.add).then_inc(taken_ready, 1)
                    own.then(eng.tensor_tensor(picked[:].rearrange("p (k t) e -> p k t e", k=TOP_K), chosen[:].rearrange("p (k t) e -> p k t e", k=TOP_K),
                                               place[:].unsqueeze(1).broadcast_to([P, TOP_K, TPB, EXPERTS]), ALU.mult))
                    own.settle(r)
                    own.then(eng.tensor_reduce(own_place[:], picked[:], AX_X, ALU.add))
                    own.settle(r)

                def make_entries(r, k):
                    flat_choice = choice[:].rearrange("p k t -> p (k t)")
                    own.then(eng.tensor_scalar(past[:], own_place[:], float(CAPACITY), float(FAR), ALU.is_ge, ALU.mult))
                    own.then(eng.scalar_tensor_tensor(slot_f[:], flat_choice, float(CAPACITY), own_place[:], ALU.mult, ALU.add))
                    eng.wait_ge(second_ready, r + 1)
                    own.then(eng.tensor_scalar(total[:], second[:], 1.0, None, ALU.add))
                    own.settle(r)
                    own.then(eng.tensor_tensor(slot[k][:], slot_f[:], past[:], ALU.add))
                    own.then(eng.reciprocal(total[:], total[:]))
                    own.settle(r)
                    own.then(eng.tensor_scalar(rows[k][:, :, WEIGHT], total[:], ffn_gate[:], None, ALU.mult))
                    own.then(eng.tensor_copy(rows[k][:, :, TOKEN].bitcast(I32), token[:]))
                    own.then(eng.tensor_copy(rows[k][:, :, CHOICE:CHOICE + TOP_K], choice[:].rearrange("p k t -> p t k")))
                    own.settle(r)
                    own.then(eng.tensor_scalar(token[:], token[:], float(SEQ), None, ALU.add))
                    eng.tensor_tensor(rows[k][:, :, WEIGHT + 1], rows[k][:, :, WEIGHT], second[:], ALU.mult).then_inc(routed, 1)
                    assert own.done == STEPS, own.done

                def raise_flag(g):
                    eng.wait_ge(taken_ready, GROUP * g + 1)
                    eng.tensor_reduce(least[:], taken[:], AX_X, ALU.min).then_inc(least_ready, 1)
                    eng.wait_ge(least_ready, g)
                    eng.tensor_scalar(active[:], least[:], float(CAPACITY), None, ALU.is_lt).then_inc(flag_ready, 1)

                def route_step(b, k, t):
                    if there(b - 1):
                        r_stat(b - 1, (k - 1) % GROUP, t)
                    if t == 0 and there(b - 2):
                        r_shifts(b - 2, (k - 2) % GROUP)
                    if there(b - 3):
                        if t > 0:
                            (choose, find_places, make_entries)[t - 1](b - 3, (k - 3) % GROUP)
                    if t == TPB - 1 and there(b - 1):
                        r_spreads(b - 1, (k - 1) % GROUP)

                eng.wait_ge(marks_loaded, 3 * DMA)
                eng.wait_ge(const_set, 4)
                eng.tensor_copy(lens[:], lens_i[:]).then_inc(prep, 1)
                eng.wait_ge(prep, 1)
                own_ends = ends[:, 0:PATCHES]
                eng.tensor_tensor_scan(own_ends, lens[:], nothing[:], -1.0, ALU.add, ALU.add).then_inc(prep, 1)
                eng.wait_ge(prep, 2)
                eng.tensor_scalar(wraps[:], own_ends, 0.0, float(SEQ), ALU.is_lt, ALU.mult).then_inc(prep, 1)
                eng.wait_ge(prep, 3)
                eng.tensor_tensor(own_ends, own_ends, wraps[:], ALU.add).then_inc(prep, 1)
                eng.wait_ge(prep, 4)

                def mark(p, i):
                    wait_count(eng, marked, p - 1)
                    eng.scalar_tensor_tensor(marks[i][:], pos[:], ends[:, bass.ds(p, 1)], marks[i][:],
                                             ALU.is_equal, ALU.max).then_inc(marked, 1)

                for p in range(2 * MARKS):
                    mark(p, p % 2)
                stats(0, 1, 0, range(TPB))
                spreads(0, 0)
                with eng.Fori(2, 6) as m:
                    for i in range(MARKS):
                        mark(MARKS * m + i, i % 2)
                shifts(0, 0)
                eng.wait_ge(const_loaded, CONSTS)
                patches(0, 0)
                stats(1, 1, 1, range(TPB))
                spreads(1, 1)
                with eng.Fori(6, ROWS // MARKS) as m:
                    for i in range(MARKS):
                        mark(MARKS * m + i, i % 2)
                eng.wait_ge(marked, ROWS)
                eng.tensor_tensor(marks[0][:], marks[0][:], marks[1][:], ALU.max).then_inc(prep, 1)
                eng.wait_ge(prep, 5)
                eng.tensor_tensor_scan(ended[:], marks[0][:], marks[0][:], 0.0, ALU.add, ALU.max).then_inc(ended_ready, 1)
                eng.wait_ge(ended_ready, 1)
                eng.wait_ge(carried, 1)
                eng.tensor_scalar(plug[:], ended[:], ps_c[:, 0:1], None, ALU.add).then_inc(plug_ready, 1)
                shifts(1, 1)
                lo_pool(0, 0)
                lo_tile(0, 0)
                eng.wait_ge(gate_ready, 2)
                onehots(0, 1, 0)

                def turn(g, routing, last):
                    for k in range(GROUP):
                        b = GROUP * g + k
                        nk, ak = (k + 1) % GROUP, (k + 2) % GROUP
                        end = last and k == GROUP - 1
                        for t in range(TPB):
                            n = TPB * b + t
                            if not (end and t == TPB - 1):
                                lo_tile(n + 1, (t + 1) % 2)
                            if not (last and k >= GROUP - 2):
                                stats(b + 2, g + 1 + (k + 2) // GROUP, ak, (t,))
                            if t == 0 and not end and not (isinstance(b, int) and b == 0):
                                shifts(b + 1, nk)
                            if t == 0 and not end:
                                patches(b + 1, nk)
                                onehots(b + 1, g + 1 + (k + 1) // GROUP, nk)
                            if routing:
                                route_step(b, k, t)
                            if t == TPB - 1:
                                if not (last and k >= GROUP - 2):
                                    spreads(b + 2, ak)
                                if not end:
                                    lo_pool(b + 1, nk)
                            add_tile(n, g, k, t)
                    if routing and not (isinstance(g, int) and g == 0):
                        raise_flag(g)
                        hold(eng, flag_ready, g, passed)

                def after(b, k):
                    for t in range(TPB):
                        route_step(b, k, t)

                turns(eng, turn, after)


def experts(nc, io, x1_dram, tokens_dram):
    W_in, W_gate, W_out = io["W"], io["V"], io["W_out"]
    x1_rows = x1_dram.rearrange("b s d -> (b s) d")
    tok_rows = tokens_dram.rearrange("(e p t) d -> e p t d", e=EXPERTS, t=ET)
    meta = tokens_dram.rearrange("(e p t) d -> e p t d", e=EXPERTS, t=ET)[:, :, :, D:ROW]
    QC = 2
    HALF = CAPACITY // 2
    with ExitStack() as ctx:
        def sb(name, shape, dt=F32):
            return ctx.enter_context(nc.sbuf_tensor(name, shape, dt))

        def ps(name, shape):
            return ctx.enter_context(nc.psum_tensor(name, shape, F32))

        def sem(name):
            return ctx.enter_context(nc.semaphore(name))

        eye = sb("e_eye", [P, P])
        lists = sb("lists", [P, EXPERTS, ET * META])
        list_expert = sb("list_expert", [P, EXPERTS * ET])
        is_own = sb("is_own", [P, TOP_K, EXPERTS * ET])
        own_w = sb("own_w", [P, EXPERTS * ET])
        this_ids = sb("this_ids", [P, ET], I32)
        this_w = sb("this_w", [P, ET])
        h_hi = sb("h_hi", [P, HC, CAPACITY], F32R)
        h_lo = sb("h_lo", [P, HC, CAPACITY], F32R)
        t_hi = sb("t_hi", [P, KC, CAPACITY], F32R)
        t_lo = sb("t_lo", [P, KC, CAPACITY], F32R)
        o_hi = sb("o_hi", [P, HC, D], F32R)
        o_lo = sb("o_lo", [P, HC, D], F32R)
        o_raw = [sb(f"o_raw{i}", [P, D]) for i in range(4)]
        wv_raw = [sb(f"wv_raw{i}", [P, 2, KC, QC * P]) for i in range(2)]
        wv_hi = [sb(f"wv_hi{i}", [P, 2, KC, P], F32R) for i in range(2)]
        wv_lo = [sb(f"wv_lo{i}", [P, 2, KC, P], F32R) for i in range(2)]
        silu = [sb(f"silu{i}", [P, HALF]) for i in range(2)]
        prod = [sb(f"prod{i}", [P, HALF]) for i in range(2)]
        tok = [sb(f"tok{i}", [P, D]) for i in range(4)]
        acc = [sb(f"acc{i}", [P, D]) for i in range(4)]
        new = [sb(f"new{i}", [P, D]) for i in range(2)]

        ps_g = [ps(f"ps_g{i}", [P, HALF]) for i in range(2)]
        ps_a = [ps(f"ps_a{i}", [P, HALF]) for i in range(2)]
        ps_y = [ps(f"ps_y{i}", [P, D]) for i in range(2)]
        ps_t = [ps(f"e_ps_t{i}", [P, D]) for i in range(2)]

        const_loaded = sem("e_const_loaded")
        eye_loaded = sem("eye_loaded")
        CONSTS = (1 + EXPERTS) * DMA
        cleared = sem("cleared")
        wv_loaded = [sem(f"wv_loaded{i}") for i in range(2)]
        o_loaded = [sem(f"o_loaded{i}") for i in range(4)]
        ids_ready = sem("ids_ready")
        weights_ready = sem("weights_ready")
        own_steps = sem("own_steps")
        tok_loaded = [sem(f"tok_loaded{i}") for i in range(4)]
        acc_gathered = [sem(f"acc_gathered{i}") for i in range(4)]
        scattered = [sem(f"scattered{i}") for i in range(2)]
        wv_hi_ready = sem("wv_hi_ready")
        wv_lo_ready = sem("wv_lo_ready")
        o_hi_ready = sem("o_hi_ready")
        o_lo_ready = sem("o_lo_ready")
        gated = sem("gated")
        raised = sem("raised")
        silu_ready = sem("silu_ready")
        prod_ready = sem("prod_ready")
        h_hi_ready = sem("h_hi_ready")
        h_lo_ready = sem("h_lo_ready")
        turned = sem("e_turned")
        t_hi_ready = sem("t_hi_ready")
        t_lo_ready = sem("t_lo_ready")
        lowered = sem("lowered")
        new_ready = sem("new_ready")
        passed = sem("passed")

        def loop(eng, body):
            body(0, False)
            with eng.Fori(1, EXPERTS - 1) as e:
                body(e, False)
            body(EXPERTS - 1, True)

        with nc.Block() as block:

            @block.sync
            def _(eng):
                eng.dma_start(eye[:], io["c_eye"]).then_inc(eye_loaded, DMA)

                def load_tile(e, t):
                    wait_count(eng, turned, ET * e + t - 3)
                    eng.dma_start(tok[t % 4][:], tok_rows[e][:, t, 0:D]).then_inc(tok_loaded[t % 4], DMA)

                def load_weights(e, q):
                    i = q % 2
                    quarter = HC // QC * e + q
                    wait_count(eng, wv_hi_ready, QC * (quarter - 1))
                    wait_count(eng, wv_lo_ready, QC * (quarter - 1))
                    for m, w in enumerate((W_in, W_gate)):
                        src = w[e][:, q * QC * P:(q + 1) * QC * P].rearrange("(c p) h -> p c h", p=P)
                        eng.dma_start(wv_raw[i][:, m], src).then_inc(wv_loaded[i], DMA)
                    for h in range(QC * q, QC * (q + 1)):
                        wait_count(eng, o_hi_ready, HC * e + h - 3)
                        wait_count(eng, o_lo_ready, HC * e + h - 3)
                        eng.dma_start(o_raw[h % 4][:], W_out[e][h * P:(h + 1) * P, :]).then_inc(o_loaded[h % 4], DMA)

                for t in range(4):
                    load_tile(0, t)
                load_weights(0, 0)
                for t in range(4, ET):
                    load_tile(0, t)
                eng.dma_start(list_expert[:], io["c_list_expert"]).then_inc(const_loaded, DMA)
                for e in range(EXPERTS):
                    eng.dma_start(lists[:, e].rearrange("p (t w) -> p t w", w=META), meta[e]).then_inc(const_loaded, DMA)

                def body(e, last):
                    for q in range(1, HC // QC):
                        load_weights(e, q)
                    if not last:
                        load_weights(e + 1, 0)
                        for t in range(ET):
                            load_tile(e + 1, t)

                loop(eng, body)

            @block.gpsimd
            def _(eng):
                bound = dict(bounds_check=TOKENS - 1, oob_is_err=False)

                def gather_acc(n, t, first):
                    if not first:
                        hold(eng, new_ready, n - 3, passed)
                    eng.indirect_dma_start(acc[t % 4][:], None, x1_rows, bass.IndirectOffsetOnAxis(this_ids[:, t:t + 1], 0),
                                           **bound).then_inc(acc_gathered[t % 4], DMA)

                def scatter(n, t):
                    hold(eng, new_ready, n + 1, passed)
                    eng.indirect_dma_start(x1_rows, bass.IndirectOffsetOnAxis(this_ids[:, t:t + 1], 0), new[t % 2][:], None,
                                           **bound).then_inc(scattered[t % 2], DMA)

                eng.wait_ge(const_loaded, CONSTS)
                eng.wait_ge(cleared, 1)

                def body(e, last):
                    own = lists[:, bass.ds(e, 1), :].rearrange("p o (t w) -> p (o t) w", w=META)[:, :, TOKEN - D].bitcast(I32)
                    for i in range(2):
                        if not isinstance(e, int) or e > 0:
                            hold(eng, scattered[i], DMA * (ET // 2) * e, passed)
                    eng.tensor_copy(this_ids[:], own).then_inc(ids_ready, 1)
                    hold(eng, ids_ready, e + 1, passed)
                    for t in range(4):
                        gather_acc(ET * e + t, t, isinstance(e, int) and e == 0)
                    for t in range(ET):
                        scatter(ET * e + t, t)
                        if t + 4 < ET:
                            gather_acc(ET * e + t + 4, t + 4, False)

                loop(eng, body)
                for i in range(2):
                    eng.wait_ge(scattered[i], DMA * (ET // 2) * EXPERTS)

            @block.tensor
            def _(eng):
                def turn_tile(n, turn_no, t):
                    eng.wait_ge(tok_loaded[t % 4], DMA * (2 * turn_no + t // 4 + 1))
                    wait_count(eng, t_hi_ready, n - 1)
                    wait_count(eng, t_lo_ready, n - 1)
                    for c in range(KC):
                        mm = eng.transpose(ps_t[t % 2][:, c * P:(c + 1) * P], tok[t % 4][:, c * P:(c + 1) * P], eye[:])
                    mm.then_inc(turned, 1)

                def product(out, stationary, moving, i, first, last):
                    (s_hi, s_lo), (m_hi, m_lo) = stationary, moving
                    eng.matmul(out, s_hi, m_hi, start=first, stop=False)
                    eng.matmul(out, s_hi, m_lo, start=False, stop=False)
                    return eng.matmul(out, s_lo, m_hi, start=False, stop=last)

                def raise_half(out, m, i, half):
                    cols = slice(half * HALF, (half + 1) * HALF)
                    for c in range(KC):
                        mm = product(out, (wv_hi[i][:, m, c, :], wv_lo[i][:, m, c, :]),
                                     (t_hi[:, c, cols], t_lo[:, c, cols]), c, c == 0, c == KC - 1)
                    return mm

                eng.wait_ge(eye_loaded, DMA)
                for t in range(ET):
                    turn_tile(t, 0, t)

                def body(e, last):
                    eng.wait_ge(t_hi_ready, ET * (e + 1))
                    eng.wait_ge(t_lo_ready, ET * (e + 1))
                    for h in range(HC):
                        chunk = HC * e + h
                        eng.wait_ge(wv_hi_ready, chunk + 1)
                        eng.wait_ge(wv_lo_ready, chunk + 1)
                        for s in range(2):
                            wait_count(eng, silu_ready, 2 * chunk + s - 1)
                            raise_half(ps_g[s][:], 1, h % 2, s).then_inc(gated, 1)
                            wait_count(eng, prod_ready, 2 * chunk + s - 1)
                            raise_half(ps_a[s][:], 0, h % 2, s).then_inc(raised, 1)
                    for t in range(ET):
                        if not last:
                            turn_tile(ET * (e + 1) + t, e + 1, t)
                        wait_count(eng, new_ready, ET * e + t - 1)
                        rows = slice(t * P, (t + 1) * P)
                        for h in range(HC):
                            if t == 0:
                                eng.wait_ge(h_hi_ready, 2 * (HC * e + h) + 1)
                                eng.wait_ge(h_lo_ready, 2 * (HC * e + h) + 1)
                                eng.wait_ge(o_hi_ready, HC * e + h + 1)
                                eng.wait_ge(o_lo_ready, HC * e + h + 1)
                            if t == ET // 2 and h == 0:
                                eng.wait_ge(h_hi_ready, 2 * HC * (e + 1))
                                eng.wait_ge(h_lo_ready, 2 * HC * (e + 1))
                            mm = product(ps_y[t % 2][:], (h_hi[:, h, rows], h_lo[:, h, rows]),
                                         (o_hi[:, h, :], o_lo[:, h, :]), h, h == 0, h == HC - 1)
                        mm.then_inc(lowered, 1)

                loop(eng, body)

            @block.scalar
            def _(eng):
                def split_wv(chunk, quarter_turn, h):
                    q = h // QC
                    eng.wait_ge(wv_loaded[q % 2], 2 * DMA * (2 * quarter_turn + q // 2 + 1))
                    wait_count(eng, raised, 2 * (chunk - 1))
                    cols = slice(h % QC * P, (h % QC + 1) * P)
                    eng.activation(wv_hi[h % 2][:].rearrange("p m c h -> p (m c) h"), wv_raw[q % 2][:, :, :, cols].rearrange("p m c h -> p (m c) h"),
                                   ACT.Copy).then_inc(wv_hi_ready, 1)

                def split_list_tile(e, t):
                    eng.wait_ge(turned, ET * e + t + 1)
                    if t == 0:
                        wait_count(eng, raised, 2 * HC * e)
                    eng.activation(t_hi[:, :, t * P:(t + 1) * P], ps_t[t % 2][:].rearrange("p (c s) -> p c s", c=KC),
                                   ACT.Copy).then_inc(t_hi_ready, 1)

                split_wv(0, 0, 0)
                for t in range(ET):
                    split_list_tile(0, t)

                def body(e, last):
                    for h in range(HC):
                        chunk = HC * e + h
                        if h + 1 < HC:
                            split_wv(chunk + 1, e, h + 1)
                        elif not last:
                            split_wv(chunk + 1, e + 1, 0)
                        eng.wait_ge(o_loaded[h % 4], DMA * (2 * e + h // 4 + 1))
                        if h == 0:
                            wait_count(eng, lowered, ET * e)
                        eng.activation(o_hi[:, h, :], o_raw[h % 4][:], ACT.Copy).then_inc(o_hi_ready, 1)
                        for s in range(2):
                            eng.wait_ge(gated, 2 * chunk + s + 1)
                            wait_count(eng, prod_ready, 2 * chunk + s - 1)
                            eng.activation(silu[s][:], ps_g[s][:], ACT.Silu).then_inc(silu_ready, 1)
                            eng.wait_ge(prod_ready, 2 * chunk + s + 1)
                            eng.activation(h_hi[:, h, s * HALF:(s + 1) * HALF], prod[s][:], ACT.Copy).then_inc(h_hi_ready, 1)
                    if not last:
                        for t in range(ET):
                            split_list_tile(e + 1, t)

                loop(eng, body)

            @block.vector
            def _(eng):
                for i in range(3):
                    eng.memset(acc[i][:], 0.0)
                eng.memset(acc[3][:], 0.0).then_inc(cleared, 1)
                def split_wv(chunk, h):
                    q = h // QC
                    eng.wait_ge(wv_hi_ready, chunk + 1)
                    cols = slice(h % QC * P, (h % QC + 1) * P)
                    eng.tensor_tensor(wv_lo[h % 2][:].rearrange("p m c h -> p (m c) h"), wv_raw[q % 2][:, :, :, cols].rearrange("p m c h -> p (m c) h"),
                                      wv_hi[h % 2][:].bitcast(F32).rearrange("p m c h -> p (m c) h"), ALU.subtract).then_inc(wv_lo_ready, 1)

                def split_list_tile(e, t):
                    cols = slice(t * P, (t + 1) * P)
                    eng.wait_ge(t_hi_ready, ET * e + t + 1)
                    eng.tensor_tensor(t_lo[:, :, cols], ps_t[t % 2][:].rearrange("p (c s) -> p c s", c=KC),
                                      t_hi[:, :, cols].bitcast(F32), ALU.subtract).then_inc(t_lo_ready, 1)

                split_wv(0, 0)
                for t in range(ET):
                    split_list_tile(0, t)
                eng.wait_ge(const_loaded, CONSTS)
                word = lists[:].rearrange("p e (t w) -> p (e t) w", w=META)
                for i in range(TOP_K):
                    eng.tensor_tensor(is_own[:, i], word[:, :, CHOICE - D + i], list_expert[:], ALU.is_equal).then_inc(own_steps, 1)
                for i in range(TOP_K):
                    eng.wait_ge(own_steps, i + 1)
                    eng.tensor_tensor(is_own[:, i], is_own[:, i], word[:, :, WEIGHT - D + i], ALU.mult).then_inc(own_steps, 1)
                eng.wait_ge(own_steps, 2 * TOP_K)
                eng.tensor_tensor(own_w[:], is_own[:, 0], is_own[:, 1], ALU.add).then_inc(own_steps, 1)
                eng.wait_ge(own_steps, 2 * TOP_K + 1)

                def body(e, last):
                    if not isinstance(e, int) or e > 0:
                        hold(eng, new_ready, ET * e, passed)
                    eng.tensor_copy(this_w[:], own_w[:, bass.ds(e * ET, ET)]).then_inc(weights_ready, 1)
                    for h in range(HC):
                        chunk = HC * e + h
                        if h + 1 < HC:
                            split_wv(chunk + 1, h + 1)
                        elif not last:
                            split_wv(chunk + 1, 0)
                        eng.wait_ge(o_hi_ready, chunk + 1)
                        eng.tensor_tensor(o_lo[:, h, :], o_raw[h % 4][:], o_hi[:, h, :].bitcast(F32), ALU.subtract).then_inc(o_lo_ready, 1)
                        for s in range(2):
                            cols = slice(s * HALF, (s + 1) * HALF)
                            eng.wait_ge(silu_ready, 2 * chunk + s + 1)
                            eng.wait_ge(raised, 2 * chunk + s + 1)
                            wait_count(eng, h_hi_ready, 2 * chunk + s - 1)
                            eng.tensor_tensor(prod[s][:], ps_a[s][:], silu[s][:], ALU.mult).then_inc(prod_ready, 1)
                            eng.wait_ge(h_hi_ready, 2 * chunk + s + 1)
                            eng.tensor_tensor(h_lo[:, h, cols], prod[s][:], h_hi[:, h, cols].bitcast(F32), ALU.subtract).then_inc(h_lo_ready, 1)
                    eng.wait_ge(weights_ready, e + 1)
                    for t in range(ET):
                        if not last:
                            split_list_tile(e + 1, t)
                        eng.wait_ge(acc_gathered[t % 4], DMA * (2 * e + t // 4 + 1))
                        wait_count(eng, scattered[t % 2], DMA * (ET // 2 * e + t // 2))
                        eng.wait_ge(lowered, ET * e + t + 1)
                        eng.scalar_tensor_tensor(new[t % 2][:], ps_y[t % 2][:], this_w[:, t:t + 1], acc[t % 4][:],
                                                 ALU.mult, ALU.add).then_inc(new_ready, 1)

                loop(eng, body)


def kernel(**inputs):
    from concourse import bacc
    from concourse.bass_utils import run_bass_kernel_spmd

    x = np.asarray(inputs["x"])
    laid_out = {
        "x": x,
        "ctx": np.asarray(inputs["ctx_2048"]),
        "lens": np.asarray(inputs["mask_BxS2_if0"]),
        "g_xattn": np.asarray(inputs["g_xattn"]),
        "g_ffn": np.asarray(inputs["g_ffn"]),
        "w_in": np.asarray(inputs["L0_xattn_W_in"]).T,
        "b_in": np.asarray(inputs["L0_xattn_b_in"]).reshape(1, D),
        "gain_res": np.asarray(inputs["L0_xattn_g_res"]).reshape(KC, P).T,
        "gain_ctx": np.asarray(inputs["L0_xattn_g_init"]),
        "router_w": np.asarray(inputs["L0_ffn_router_w"]).T,
        "router_b": np.asarray(inputs["L0_ffn_router_b"]),
        "W": np.asarray(inputs["L0_ffn_W"]),
        "V": np.asarray(inputs["L0_ffn_V"]),
        "W_out": np.asarray(inputs["L0_ffn_W_out"]),
        **constants(),
    }
    nc = bacc.Bacc("TRN2", target_bir_lowering=False, num_devices=1)
    arrays, io = {}, {}
    for name, a in laid_out.items():
        arrays[f"in_{name}"] = np.ascontiguousarray(a)
        io[name] = nc.dram_tensor(f"in_{name}", a.shape, mybir.dt.from_np(a.dtype), kind="ExternalInput").ap()
    out = nc.dram_tensor("out_x", [BATCH, SEQ, D], F32, kind="ExternalOutput").ap()
    build(nc, io, out)
    result = run_bass_kernel_spmd(nc, [arrays], core_ids=[0])
    return result.results[0]["out_x"]


def build(nc, io, out):
    tokens_dram = nc.dram_tensor("tokens_dram", [EXPERTS * CAPACITY, ROW], F32, kind="Internal").ap()
    mix(nc, io, out, tokens_dram)
    experts(nc, io, out, tokens_dram)
```

```python
from contextlib import ExitStack

import numpy as np
import concourse.bass as bass
from concourse import mybir

F32 = mybir.dt.float32
F32R = mybir.dt.float32r
F16 = mybir.dt.float16
I32 = mybir.dt.int32
U32 = mybir.dt.uint32
ALU = mybir.AluOpType
ACT = mybir.ActivationFunctionType
AX_X = mybir.AxisListType.X

P = 128
BATCH, SEQ, D = 64, 512, 512
TOKENS = BATCH * SEQ
PATCHES, D_CTX = 77, 1024
HIDDEN, EXPERTS, TOP_K = 1024, 8, 2
CAPACITY = 2 * 2048 * TOP_K // EXPERTS
EPS = 1e-5
KC = D // P
TPB = SEQ // P
HC = HIDDEN // P
ET = CAPACITY // P
ROWS = PATCHES + 1
GROUP = 4
META = 8
TOKEN, WEIGHT, CHOICE = D, D + 1, D + 3
ROW = D + META
QC = 2
FAR = 32768
DMA = 16

_LOGP = np.float32(-0.001)
_DT = -np.log(-np.expm1(_LOGP.astype(np.float64)))


def wait_count(eng, sem, count):
    if not isinstance(count, int) or count > 0:
        eng.wait_ge(sem, count)


def hold(eng, sem, count, passed):
    eng.wait_ge(sem, count)
    eng.sem_inc(passed)


def constants():
    decay = np.zeros((ROWS, ROWS))
    q, p = np.meshgrid(np.arange(PATCHES), np.arange(PATCHES))
    decay[:PATCHES, :PATCHES] = np.where(q >= p, np.exp(_LOGP) * np.exp(-_DT * np.maximum(q - p, 0)), 0.0)
    decay[PATCHES, PATCHES] = 1.0
    at = np.arange(P)
    carry = np.zeros((P, P), np.float32)
    carry[at[:BATCH], at[:BATCH] + BATCH] = 1.0
    blank = np.zeros((P, ROW), np.int32)
    blank[:, TOKEN] = TOKENS
    return {
        "c_eye": np.eye(P, dtype=np.float32),
        "c_eye16": np.eye(P, dtype=np.float16),
        "c_decay": decay.astype(np.float32),
        "c_rank": np.arange(1, PATCHES + 1, dtype=np.float32)[:, None],
        "c_pos": (np.arange(SEQ // 2)[None, :] + np.where(at < BATCH, 0, SEQ // 2)[:, None]).astype(np.float16),
        "c_carry": carry,
        "c_before": (at[:, None] < at[None, :]).astype(np.float16),
        "c_expert": np.broadcast_to(np.arange(EXPERTS, dtype=np.float32), (P, EXPERTS)),
        "c_token": (np.arange(TPB)[None, :] * P + at[:, None]).astype(np.float32),
        "c_blank": blank.view(np.float32),
        "c_place": (np.arange(ET)[None, :] * P + at[:, None]).astype(np.float32),
        "c_slot": (np.arange(EXPERTS * ET)[None, :] * P + at[:, None]).astype(np.float32),
        "c_list_expert": np.broadcast_to(np.repeat(np.arange(EXPERTS, dtype=np.float32), ET), (P, EXPERTS * ET)),
    }


class Shared:

    def __init__(self, nc, ctx):
        self.eye = ctx.enter_context(nc.sbuf_tensor("eye", [P, P], F32))
        self.weights = ctx.enter_context(nc.sbuf_tensor("weights", [P, KC * D], F32))
        self.first_loaded = ctx.enter_context(nc.semaphore("wv_loaded0"))
        self.x1_stored = [ctx.enter_context(nc.semaphore(f"x1_stored{i}")) for i in range(GROUP)]


def load_quarter(eng, io, wv, e, q, loaded):
    for m, w in enumerate((io["W"], io["V"])):
        src = w[e][:, q * QC * P:(q + 1) * QC * P].rearrange("(c p) h -> p c h", p=P)
        eng.dma_start(wv[:, m], src).then_inc(loaded, DMA)


def mix(nc, io, x1_dram, tokens_dram, shared):
    MARKS = 13
    with ExitStack() as ctx:
        def sb(name, shape, dt=F32):
            return ctx.enter_context(nc.sbuf_tensor(name, shape, dt))

        def ps(name, shape):
            return ctx.enter_context(nc.psum_tensor(name, shape, F32))

        def sem(name):
            return ctx.enter_context(nc.semaphore(name))

        eye = shared.eye
        decay = sb("decay", [ROWS, ROWS])
        decay_hi = sb("decay_hi", [ROWS, ROWS], F32R)
        decay_lo = sb("decay_lo", [ROWS, ROWS], F32R)
        lens_i = sb("lens_i", [P, PATCHES], I32)
        lens = sb("lens", [P, PATCHES])
        nothing = sb("nothing", [P, PATCHES])
        ends = sb("ends", [P, ROWS])
        wraps = sb("wraps", [P, PATCHES])
        pos = sb("pos", [P, SEQ // 2], F16)
        is_end = [sb(f"is_end{i}", [P, SEQ // 2], F16) for i in range(MARKS)]
        eye16 = sb("eye16", [P, P], F16)
        marks = sb("marks", [P, SEQ // 2], F16)
        carry = sb("carry", [P, P])
        ended = sb("ended", [P, SEQ // 2])
        plug = sb("plug", [P, SEQ // 2], F16)
        rank = sb("rank", [PATCHES, 1])
        gate_in = sb("gate_in", [P, 1])
        gate = sb("gate", [P, 1])
        gain_res = sb("gain_res", [P, KC])
        gain_ctx = sb("gain_ctx", [PATCHES, D])
        half = sb("half", [P, 5])
        blank = sb("blank", [P, ROW])
        w_raw = shared.weights[:].rearrange("p (c e) -> p c e", c=KC)
        w_hi = sb("w_hi", [P, KC, D], F32R)
        w_lo = sb("w_lo", [P, KC, D], F32R)
        x_in = [sb(f"x_in{i}", [P, TPB, D]) for i in range(GROUP)]
        c_in = [sb(f"c_in{i}", [PATCHES, D_CTX]) for i in range(GROUP)]
        p_in = [sb(f"p_in{i}", [PATCHES, SEQ], F16) for i in range(GROUP)]
        x1 = [sb(f"x1_{i}", [P, TPB, D]) for i in range(GROUP)]
        tile_stats = [sb(f"tile_stats{i}", [P, TPB, 6]) for i in range(2)]
        moments = [sb(f"moments{i}", [P, TPB, 2]) for i in range(2)]
        spread = [sb(f"spread{i}", [P, 5]) for i in range(2)]
        scale = [sb(f"scale{i}", [P, 5]) for i in range(2)]
        shift = [sb(f"shift{i}", [P, TPB]) for i in range(2)]
        squares = sb("squares", [PATCHES, D_CTX])
        sumsq = [sb(f"sumsq{i}", [PATCHES, 1]) for i in range(2)]
        patch = [sb(f"patch{i}", [ROWS, D]) for i in range(2)]
        patch_hi = [sb(f"patch_hi{i}", [ROWS, D], F32R) for i in range(2)]
        patch_lo = [sb(f"patch_lo{i}", [ROWS, D], F32R) for i in range(2)]
        pool_hi = [sb(f"pool_hi{i}", [ROWS, D], F32R) for i in range(2)]
        pool_lo = [sb(f"pool_lo{i}", [ROWS, D], F32R) for i in range(2)]
        onehot = [sb(f"onehot{i}", [ROWS, SEQ], F32R) for i in range(2)]
        xn = [sb(f"xn{i}", [P, D]) for i in range(2)]
        xt_hi = [sb(f"xt_hi{i}", [P, D], F32R) for i in range(2)]
        xt_lo = [sb(f"xt_lo{i}", [P, D], F32R) for i in range(2)]

        before = sb("before", [P, P], F16)
        all_ones = sb("all_ones", [P, P], F16)
        expert_id = sb("expert_id", [P, EXPERTS])
        router_w = sb("router_w", [P, KC, EXPERTS])
        router_b = sb("router_b", [P, EXPERTS])
        ffn_gate_in = sb("ffn_gate_in", [P, 1])
        ffn_gate = sb("ffn_gate", [P, 1])
        token = sb("token", [P, TPB])
        rows = [sb(f"rows{i}", [P, TPB, ROW]) for i in range(GROUP)]
        r_stats = [sb(f"r_stats{i}", [P, TPB, 6]) for i in range(2)]
        r_moments = [sb(f"r_moments{i}", [P, TPB, 2]) for i in range(2)]
        r_spread = [sb(f"r_spread{i}", [P, TPB]) for i in range(2)]
        r_scale = [sb(f"r_scale{i}", [P, TPB]) for i in range(2)]
        r_shift = [sb(f"r_shift{i}", [P, TPB]) for i in range(2)]
        r_xt = [sb(f"r_xt{i}", [P, D]) for i in range(2)]
        logits = sb("logits", [P, TPB, EXPERTS])
        top = sb("top", [P, TPB, 8])
        top_at = sb("top_at", [P, TPB, 8], U32)
        gap = sb("gap", [P, TPB])
        second = sb("second", [P, TPB])
        total = sb("total", [P, TPB])
        choice = sb("choice", [P, TOP_K, TPB])
        chosen = sb("chosen", [P, TOP_K * TPB, EXPERTS])
        either = sb("either", [P, TPB * EXPERTS], F16)
        taken = sb("taken", [P, EXPERTS])
        place = sb("place", [P, TPB, EXPERTS])
        picked = sb("picked", [P, TOP_K * TPB, EXPERTS])
        own_place = sb("own_place", [P, TOP_K * TPB])
        past = sb("past", [P, TOP_K * TPB])
        slot_f = sb("slot_f", [P, TOP_K * TPB])
        slot = [sb(f"slot{i}", [P, TOP_K * TPB], I32) for i in range(GROUP)]
        list_place = sb("list_place", [P, ET])
        list_slot = sb("list_slot", [P, EXPERTS * ET])
        is_taken = sb("is_taken", [P, EXPERTS, ET])
        free_slot = sb("free_slot", [P, EXPERTS * ET], I32)
        least = sb("least", [P, 1])
        active = sb("active", [P, 1], I32)

        ps_t = [ps(f"ps_t{i}", [P, D]) for i in range(2)]
        ps_o = [ps(f"ps_o{i}", [P, D]) for i in range(2)]
        ps_d = ps("ps_d", [P, D])
        ps_r = ps("ps_r", [P, D])
        ps_s = ps("ps_s", [P, TPB * EXPERTS])
        ps_p = ps("ps_p", [P, (TPB + 1) * EXPERTS])
        ps_m, ps_c = ps_r, ps_p

        marks_loaded = sem("marks_loaded")
        const_loaded = sem("const_loaded")
        plug_stored = sem("plug_stored")
        blanked = sem("blanked")
        batch_loaded = [sem(f"batch_loaded{i}") for i in range(GROUP)]
        plug_loaded = [sem(f"plug_loaded{i}") for i in range(GROUP)]
        x1_stored = shared.x1_stored
        const_set = sem("const_set")
        prep = sem("prep")
        ends_ready = sem("ends_ready")
        marked = sem("marked")
        mark_added = sem("mark_added")
        ended_ready = sem("ended_ready")
        carried = sem("carried")
        plug_ready = sem("plug_ready")
        w_scaled = sem("w_scaled")
        w_hi_ready = sem("w_hi_ready")
        w_lo_ready = sem("w_lo_ready")
        gate_ready = sem("gate_ready")
        stats_done = sem("stats_done")
        moments_done = sem("moments_done")
        sumsq_ready = sem("sumsq_ready")
        spread_ready = sem("spread_ready")
        scale_ready = sem("scale_ready")
        shift_ready = sem("shift_ready")
        normed = sem("normed")
        turned = sem("turned")
        hi_ready = sem("hi_ready")
        lo_ready = sem("lo_ready")
        mixed = sem("mixed")
        x1_ready = sem("x1_ready")
        decay_hi_ready = sem("decay_hi_ready")
        decay_lo_ready = sem("decay_lo_ready")
        patch_ready = sem("patch_ready")
        patch_hi_ready = sem("patch_hi_ready")
        patch_lo_ready = sem("patch_lo_ready")
        pooled = sem("pooled")
        pool_hi_ready = sem("pool_hi_ready")
        pool_lo_ready = sem("pool_lo_ready")
        onehot_ready = sem("onehot_ready")
        passed = sem("passed_mix")
        r_stats_done = sem("r_stats_done")
        r_moments_done = sem("r_moments_done")
        r_spread_ready = sem("r_spread_ready")
        r_scale_ready = sem("r_scale_ready")
        r_shift_ready = sem("r_shift_ready")
        r_normed = sem("r_normed")
        r_turned = sem("r_turned")
        r_copied = sem("r_copied")
        scored = sem("scored")
        logits_ready = sem("logits_ready")
        gap_ready = sem("gap_ready")
        second_ready = sem("second_ready")
        either_ready = sem("either_ready")
        counted = sem("counted")
        taken_ready = sem("taken_ready")
        step = sem("step")
        routed = sem("routed")
        entered = [sem(f"entered{i}") for i in range(GROUP)]
        least_ready = sem("least_ready")
        flag_ready = sem("flag_ready")
        taken_compared = sem("taken_compared")
        free_ready = sem("free_ready")

        plug_dram = nc.dram_tensor("plug_dram", [BATCH, SEQ], F16, kind="Internal").ap()
        LOADS = [
            (w_raw, io["w_in"].rearrange("(c p) e -> p c e", p=P)), (gain_res, io["gain_res"]),
            (eye, io["c_eye"]), (decay, io["c_decay"]), (rank, io["c_rank"]), (carry, io["c_carry"]),
            (gain_ctx, io["gain_ctx"][0:D].partition_broadcast(PATCHES)),
            (gate_in, io["g_xattn"].partition_broadcast(P)), (blank, io["c_blank"]),
            (list_place, io["c_place"]), (list_slot, io["c_slot"]),
            (before, io["c_before"]), (expert_id, io["c_expert"]), (token, io["c_token"]),
            (router_w, io["router_w"].rearrange("(c p) e -> p c e", p=P)),
            (router_b, io["router_b"].partition_broadcast(P)), (ffn_gate_in, io["g_ffn"].partition_broadcast(P)),
        ]
        CONSTS = DMA * (len(LOADS) + 2)
        LAST = BATCH // GROUP - 1
        ENTRIES = TOP_K * TPB * DMA
        STEPS = (2 * TPB + 2) + 3 + 9

        def there(row):
            return not isinstance(row, int) or 0 <= row < BATCH

        def turns(eng, turn, after, rest=None):
            turn(0, True, False)
            turn(1, True, False)

            def flagged(body, otherwise):
                flag = eng.value_load(active[0:1, 0:1], min_val=0, max_val=1)
                with eng.If(flag > 0):
                    body()
                with eng.Else():
                    otherwise()

            with eng.Fori(2, LAST) as g:
                flagged(lambda: turn(g, True, False), lambda: turn(g, False, False))
            flagged(lambda: turn(LAST, True, True), lambda: turn(LAST, False, True))
            flag = eng.value_load(active[0:1, 0:1], min_val=0, max_val=1)
            with eng.If(flag > 0):
                for b in range(BATCH, BATCH + 3):
                    after(b, b % GROUP)
                if rest:
                    rest()

        with nc.Block() as block:

            @block.sync
            def _(eng):
                def load(b, k):
                    eng.dma_start(x_in[k][:], io["x"][b].rearrange("(t p) d -> p t d", p=P)).then_inc(batch_loaded[k], DMA)
                    eng.dma_start(c_in[k][:], io["ctx"][b]).then_inc(batch_loaded[k], DMA)

                def load_plug(b, k):
                    eng.dma_start(p_in[k][:], plug_dram[b].partition_broadcast(PATCHES)).then_inc(plug_loaded[k], DMA)

                halves = plug_dram.rearrange("b (h s) -> h b s", h=2)
                for h in range(2):
                    eng.dma_start(lens_i[h * BATCH:(h + 1) * BATCH, :], io["lens"]).then_inc(marks_loaded, DMA)
                eng.dma_start(pos[:], io["c_pos"]).then_inc(marks_loaded, DMA)
                eng.dma_start(eye16[:], io["c_eye16"]).then_inc(marks_loaded, DMA)
                load(0, 0)
                eng.wait_ge(const_set, 4)
                for i in range(2):
                    eng.dma_start(patch[i][PATCHES:ROWS, :], io["b_in"]).then_inc(const_loaded, DMA)
                eng.wait_ge(const_loaded, CONSTS)
                for k in range(1, GROUP):
                    load(k, k)
                eng.wait_ge(plug_ready, 1)
                for h in range(2):
                    eng.dma_start(halves[h], plug[h * BATCH:(h + 1) * BATCH, :]).then_inc(plug_stored, DMA)
                eng.wait_ge(plug_stored, 2 * DMA)
                for k in range(GROUP):
                    load_plug(k, k)

                def turn(g, last=False):
                    for k in range(GROUP):
                        b = GROUP * g + k
                        row_tiles = x1_dram[b].rearrange("(t p) d -> p t d", p=P)
                        if last and k == GROUP - 1:
                            eng.wait_ge(x1_ready, TPB * (b + 1) - 1)
                            eng.dma_start(row_tiles[:, 0:TPB - 1], x1[k][:, 0:TPB - 1]).then_inc(x1_stored[k], DMA)
                            eng.wait_ge(x1_ready, TPB * (b + 1))
                            eng.dma_start(row_tiles[:, TPB - 1:], x1[k][:, TPB - 1:]).then_inc(x1_stored[k], DMA)
                            continue
                        eng.wait_ge(x1_ready, TPB * (b + 1))
                        eng.dma_start(row_tiles, x1[k][:]).then_inc(x1_stored[k], DMA)
                        if not last:
                            load(b + GROUP, k)
                            load_plug(b + GROUP, k)

                turn(0)
                with eng.Fori(1, LAST) as g:
                    turn(g)
                eng.wait_ge(w_lo_ready, KC)
                load_quarter(eng, io, shared.weights[:].rearrange("p (m c h) -> p m c h", m=2, c=KC), 0, 0, shared.first_loaded)
                turn(LAST, last=True)

            @block.gpsimd
            def _(eng):
                def root(b, k):
                    eng.wait_ge(spread_ready, 2 * (b + 1))
                    wait_count(eng, normed, TPB * (b - 1))
                    eng.tensor_tensor(scale[k % 2][:], spread[k % 2][:], half[:], ALU.pow).then_inc(scale_ready, 1)

                def lo_patch(row, k):
                    eng.wait_ge(patch_hi_ready, row + 1)
                    eng.tensor_tensor(patch_lo[k % 2][:], patch[k % 2][:], patch_hi[k % 2][:].bitcast(F32), ALU.subtract).then_inc(patch_lo_ready, 1)

                def r_root(r, k):
                    eng.wait_ge(r_spread_ready, r + 1)
                    wait_count(eng, r_normed, TPB * (r - 1))
                    eng.tensor_tensor(r_scale[k % 2][:], r_spread[k % 2][:], half[:, 0:TPB], ALU.pow).then_inc(r_scale_ready, 1)

                def enter(r, k):
                    hold(eng, routed, r + 1, passed)
                    for s in range(TOP_K * TPB):
                        eng.indirect_dma_start(
                            tokens_dram, bass.IndirectOffsetOnAxis(slot[k][:, s:s + 1], 0), rows[k][:, s % TPB, :], None,
                            bounds_check=EXPERTS * CAPACITY - 1, oob_is_err=False).then_inc(entered[k], DMA)

                def route_roots(b, k):
                    if there(b - 1):
                        r_root(b - 1, (k - 1) % GROUP)

                def route_enter(b, k):
                    if there(b - 3):
                        enter(b - 3, (k - 3) % GROUP)

                eng.wait_ge(const_set, 4)
                root(0, 0)
                for c in range(KC):
                    eng.wait_ge(w_hi_ready, c + 1)
                    eng.tensor_tensor(w_lo[:, c, :], w_raw[:, c, :], w_hi[:, c, :].bitcast(F32), ALU.subtract).then_inc(w_lo_ready, 1)
                lo_patch(0, 0)
                root(1, 1)

                def turn(g, routing, last):
                    for k in range(GROUP):
                        b = GROUP * g + k
                        if not (last and k == GROUP - 1):
                            lo_patch(b + 1, (k + 1) % GROUP)
                        if not (last and k >= GROUP - 2):
                            root(b + 2, (k + 2) % GROUP)
                        if routing:
                            route_roots(b, k)
                            if k == GROUP - 1 and not (isinstance(g, int) and g == 0):
                                for i in range(GROUP):
                                    hold(eng, entered[i], ENTRIES * g, passed)
                            route_enter(b, k)
                    if routing and not (isinstance(g, int) and g == 0):
                        hold(eng, flag_ready, g, passed)

                def after(b, k):
                    route_roots(b, k)
                    route_enter(b, k)

                def fill_lists():
                    for i in range(GROUP):
                        hold(eng, entered[i], ENTRIES * (BATCH // GROUP), passed)
                    hold(eng, free_ready, 1, passed)
                    for s in range(EXPERTS * ET):
                        eng.indirect_dma_start(
                            tokens_dram, bass.IndirectOffsetOnAxis(free_slot[:, s:s + 1], 0), blank[:], None,
                            bounds_check=EXPERTS * CAPACITY - 1, oob_is_err=False).then_inc(blanked, DMA)
                    eng.wait_ge(blanked, DMA * EXPERTS * ET)

                turns(eng, turn, after, fill_lists)
                eng.drain()

            @block.tensor
            def _(eng):
                def turn_tile(n, j):
                    eng.wait_ge(normed, n + 1)
                    wait_count(eng, hi_ready, n - 1)
                    wait_count(eng, lo_ready, n - 1)
                    for c in range(KC):
                        mm = eng.transpose(ps_t[j][:, c * P:(c + 1) * P], xn[j][:, c * P:(c + 1) * P], eye[:])
                    mm.then_inc(turned, 1)

                def depool(b, k):
                    eng.wait_ge(patch_hi_ready, b + 1)
                    eng.wait_ge(patch_lo_ready, b + 1)
                    wait_count(eng, pool_hi_ready, b)
                    wait_count(eng, pool_lo_ready, b)
                    eng.matmul(ps_d[0:ROWS, :], decay_hi[:], patch_hi[k % 2][:], start=True, stop=False)
                    eng.matmul(ps_d[0:ROWS, :], decay_hi[:], patch_lo[k % 2][:], start=False, stop=False)
                    eng.matmul(ps_d[0:ROWS, :], decay_lo[:], patch_hi[k % 2][:], start=False, stop=True).then_inc(pooled, 1)

                def project(n, t, between):
                    j = t % 2
                    eng.wait_ge(hi_ready, n + 1)
                    eng.wait_ge(lo_ready, n + 1)
                    wait_count(eng, x1_ready, n - 1)
                    for c in range(KC):
                        if isinstance(n, int) and n == 0:
                            eng.wait_ge(w_lo_ready, c + 1)
                        own = slice(c * P, (c + 1) * P)
                        eng.matmul(ps_o[j][:], xt_hi[j][:, own], w_hi[:, c, :], start=c == 0, stop=False)
                        eng.matmul(ps_o[j][:], xt_hi[j][:, own], w_lo[:, c, :], start=False, stop=False)
                        eng.matmul(ps_o[j][:], xt_lo[j][:, own], w_hi[:, c, :], start=False, stop=False)
                        if c == 1:
                            between()

                def mix_tile(n, b, k, t, between):
                    j = t % 2
                    if isinstance(n, int) and n == 0:
                        project(0, 0, lambda: None)
                        project(1, 1, between)
                        eng.wait_ge(plug_ready, 1)
                    elif not (isinstance(n, int) and n == 1):
                        project(n, t, between)
                    if t == 0:
                        eng.wait_ge(onehot_ready, b + 1)
                        eng.wait_ge(pool_hi_ready, b + 1)
                        eng.wait_ge(pool_lo_ready, b + 1)
                    own = slice(t * P, (t + 1) * P)
                    eng.matmul(ps_o[j][:], onehot[k % 2][:, own], pool_hi[k % 2][:], start=False, stop=False)
                    eng.matmul(ps_o[j][:], onehot[k % 2][:, own], pool_lo[k % 2][:], start=False, stop=True).then_inc(mixed, 1)

                def route_step(b, k, t):
                    q, r = (t - 2) % TPB, (b - 3 if t < 2 else b - 2)
                    if there(r):
                        eng.wait_ge(r_copied, TPB * r + q + 1)
                        if q == 0:
                            wait_count(eng, logits_ready, r)
                        for c in range(KC):
                            mm = eng.matmul(ps_s[:, q * EXPERTS:(q + 1) * EXPERTS], r_xt[q % 2][:, c * P:(c + 1) * P],
                                            router_w[:, c, :], start=c == 0, stop=c == KC - 1)
                        mm.then_inc(scored, 1)
                    q, r = (t - 1) % TPB, (b - 3 if t < 1 else b - 2)
                    if there(r):
                        slot_k = (k - 3 if t < 1 else k - 2) % GROUP
                        eng.wait_ge(r_normed, TPB * r + q + 1)
                        wait_count(eng, r_copied, TPB * r + q)
                        for c in range(KC):
                            mm = eng.transpose(ps_r[:, c * P:(c + 1) * P], rows[slot_k][:, q, c * P:(c + 1) * P], eye[:])
                        mm.then_inc(r_turned, 1)
                    if t == 2 and there(b - 3):
                        eng.wait_ge(either_ready, b - 2)
                        wait_count(eng, taken_ready, b - 3)
                        eng.matmul(ps_p[:, 0:TPB * EXPERTS], before[:], either[:], start=True, stop=False, skip_group_check=True)
                        for d in range(1, TPB + 1):
                            mm = eng.matmul(ps_p[:, d * EXPERTS:], all_ones[:], either[:, 0:(TPB + 1 - d) * EXPERTS],
                                            start=False, stop=d == TPB, skip_group_check=True)
                        mm.then_inc(counted, 1)

                def add_marks(p, i, first=False, last=False):
                    eng.wait_ge(marked, p + 1)
                    eng.matmul(ps_m[:, 0:SEQ // 2], eye16[:], is_end[i][:], start=first, stop=last,
                               skip_group_check=True).then_inc(mark_added, 1)

                for p in range(MARKS):
                    add_marks(p, p, first=p == 0)
                with eng.Fori(1, ROWS // MARKS - 1) as m:
                    for i in range(MARKS):
                        add_marks(MARKS * m + i, i)
                turn_tile(0, 0)
                for i in range(MARKS):
                    add_marks(ROWS - MARKS + i, i, last=i == MARKS - 1)
                eng.wait_ge(decay_hi_ready, 1)
                eng.wait_ge(decay_lo_ready, 1)
                depool(0, 0)
                eng.wait_ge(ended_ready, 1)
                eng.matmul(ps_c[:, 0:1], carry[:], ended[:, SEQ // 2 - 1:], start=True, stop=True).then_inc(carried, 1)

                def turn(g, routing, last):
                    for k in range(GROUP):
                        b = GROUP * g + k
                        end = last and k == GROUP - 1
                        for t in range(TPB):
                            n = TPB * b + t
                            if not (end and t == TPB - 1):
                                turn_tile(n + 1, (t + 1) % 2)
                            if t == TPB - 1 and not end:
                                depool(b + 1, k + 1)
                            mix_tile(n, b, k, t, lambda: route_step(b, k, t) if routing else None)
                    if routing and not (isinstance(g, int) and g == 0):
                        hold(eng, flag_ready, g, passed)

                def after(b, k):
                    for t in range(TPB):
                        route_step(b, k, t)

                turns(eng, turn, after)

            @block.scalar
            def _(eng):
                for dst, src in LOADS:
                    eng.dma_start(dst[:], src).then_inc(const_loaded, DMA)

                def square_row(row, turn_no, k):
                    eng.wait_ge(batch_loaded[k], 2 * DMA * turn_no)
                    wait_count(eng, spread_ready, 2 * (row - 1))
                    wait_count(eng, sumsq_ready, row)
                    eng.activation(squares[:], c_in[k][:], ACT.Square, accum_out=sumsq[k % 2][:]).then_inc(sumsq_ready, 1)

                def hi_patch(row, k):
                    eng.wait_ge(patch_ready, row + 1)
                    eng.activation(patch_hi[k % 2][:], patch[k % 2][:], ACT.Copy).then_inc(patch_hi_ready, 1)

                def norm_tile(n, row, k, t):
                    if t == 0:
                        eng.wait_ge(shift_ready, row + 1)
                    wait_count(eng, turned, n - 1)
                    eng.activation(xn[t % 2][:], x_in[k][:, t, :], ACT.Identity, bias=shift[k % 2][:, t:t + 1],
                                   scale=scale[k % 2][:, t:t + 1]).then_inc(normed, 1)

                def hi_tile(n, j):
                    eng.wait_ge(turned, n + 1)
                    wait_count(eng, mixed, n - 1)
                    eng.activation(xt_hi[j][:], ps_t[j][:], ACT.Copy).then_inc(hi_ready, 1)

                def hi_pool(row, k):
                    eng.wait_ge(pooled, row + 1)
                    wait_count(eng, mixed, TPB * (row - 1))
                    eng.activation(pool_hi[k % 2][:], ps_d[0:ROWS, :], ACT.Copy).then_inc(pool_hi_ready, 1)

                square_row(0, 1, 0)
                eng.wait_ge(const_loaded, CONSTS)
                eng.activation(gate[:], gate_in[:], ACT.Tanh).then_inc(gate_ready, 1)
                eng.activation(ffn_gate[:], ffn_gate_in[:], ACT.Tanh).then_inc(gate_ready, 1)
                eng.activation(decay_hi[:], decay[:], ACT.Copy).then_inc(decay_hi_ready, 1)
                for c in range(KC):
                    eng.activation(w_raw[:, c, :], w_raw[:, c, :], ACT.Copy, scale=gain_res[:, c:c + 1]).then_inc(w_scaled, 1)
                for c in range(KC):
                    eng.wait_ge(w_scaled, c + 1)
                    eng.activation(w_hi[:, c, :], w_raw[:, c, :], ACT.Copy).then_inc(w_hi_ready, 1)
                norm_tile(0, 0, 0, 0)
                norm_tile(1, 0, 0, 1)
                hi_patch(0, 0)
                hi_pool(0, 0)
                hi_tile(0, 0)
                square_row(1, 1, 1)

                def route_step(g, b, k, t):
                    r = b - 2
                    if there(r):
                        slot_k = (k - 2) % GROUP
                        if t == 0:
                            eng.wait_ge(r_shift_ready, r + 1)
                            if not isinstance(r, int) or r >= GROUP:
                                eng.wait_ge(entered[slot_k], ENTRIES * (g if k >= 2 else g - 1))
                        eng.activation(rows[slot_k][:, t, 0:D], x1[slot_k][:, t, :], ACT.Identity,
                                       bias=r_shift[k % 2][:, t:t + 1], scale=r_scale[k % 2][:, t:t + 1]).then_inc(r_normed, 1)
                    q, r = (t - 1) % TPB, (b - 3 if t < 1 else b - 2)
                    if there(r):
                        eng.wait_ge(r_turned, TPB * r + q + 1)
                        wait_count(eng, scored, TPB * r + q - 1)
                        eng.activation(r_xt[q % 2][:], ps_r[:], ACT.Copy).then_inc(r_copied, 1)
                    if t == 2 and there(b - 3):
                        eng.wait_ge(gap_ready, b - 2)
                        eng.activation(second[:], gap[:], ACT.Exp).then_inc(second_ready, 1)

                def turn(g, routing, last):
                    for k in range(GROUP):
                        b = GROUP * g + k
                        nk = (k + 1) % GROUP
                        end = last and k == GROUP - 1
                        for t in range(TPB):
                            n = TPB * b + t
                            if not (end and t == TPB - 1):
                                hi_tile(n + 1, (t + 1) % 2)
                            if t + 2 < TPB:
                                norm_tile(n + 2, b, k, t + 2)
                            elif not end:
                                norm_tile(n + 2, b + 1, nk, t + 2 - TPB)
                            if t == 0 and not (last and k >= GROUP - 2):
                                square_row(b + 2, g + 1 + (k + 2) // GROUP, (k + 2) % GROUP)
                            if t == 0 and not end:
                                hi_patch(b + 1, nk)
                            if t == TPB - 1 and not end:
                                hi_pool(b + 1, nk)
                            if routing:
                                route_step(g, b, k, t)
                    if routing and not (isinstance(g, int) and g == 0):
                        hold(eng, flag_ready, g, passed)

                def after(b, k):
                    for t in range(TPB):
                        route_step(b // GROUP, b, k, t)

                turns(eng, turn, after)

            @block.vector
            def _(eng):
                for i in range(2):
                    eng.memset(spread[i][:], 1.0)
                    eng.memset(onehot[i][:].bitcast(F32), 1.0).then_inc(const_set, 1)
                eng.memset(half[:], -0.5).then_inc(const_set, 1)
                eng.memset(nothing[:], 0.0)
                eng.memset(ends[:], -1e6)
                eng.memset(taken[:], 0.0)
                eng.memset(all_ones[:], 1.0)
                for i in range(GROUP):
                    eng.memset(rows[i][:, :, CHOICE + TOP_K:], 0.0)
                eng.memset(patch[0][:], 0.0)
                eng.memset(patch[1][:], 0.0).then_inc(const_set, 1)

                def stats(row, turn_no, k, tiles):
                    if tiles[0] == 0:
                        eng.wait_ge(batch_loaded[k], 2 * DMA * turn_no)
                    for t in tiles:
                        eng.bn_stats(tile_stats[k % 2][:, t, :], x_in[k][:, t, :]).then_inc(stats_done, 1)

                def spreads(row, k):
                    hold(eng, stats_done, TPB * (row + 1), passed)
                    for t in range(TPB):
                        eng.bn_aggr(moments[k % 2][:, t, :], tile_stats[k % 2][:, t, :]).then_inc(moments_done, 1)
                    eng.wait_ge(moments_done, TPB * (row + 1))
                    eng.tensor_scalar(spread[k % 2][:, 0:TPB], moments[k % 2][:, :, 1], 1.0 + EPS, EPS * EPS,
                                      ALU.mult, ALU.add).then_inc(spread_ready, 1)
                    eng.wait_ge(sumsq_ready, row + 1)
                    eng.tensor_scalar(spread[k % 2][0:PATCHES, TPB:TPB + 1], sumsq[k % 2][:], 1.0 / D_CTX, EPS,
                                      ALU.mult, ALU.add).then_inc(spread_ready, 1)

                def shifts(row, k):
                    eng.wait_ge(scale_ready, row + 1)
                    eng.scalar_tensor_tensor(shift[k % 2][:], moments[k % 2][:, :, 0], -1.0, scale[k % 2][:, 0:TPB],
                                             ALU.mult, ALU.mult).then_inc(shift_ready, 1)

                def patches(row, k):
                    wait_count(eng, pooled, row - 1)
                    eng.scalar_tensor_tensor(patch[k % 2][0:PATCHES, :], c_in[k][:, 0:D], scale[k % 2][0:PATCHES, TPB:TPB + 1],
                                             gain_ctx[:], ALU.mult, ALU.mult).then_inc(patch_ready, 1)

                def onehots(row, turn_no, k):
                    eng.wait_ge(plug_loaded[k], DMA * turn_no)
                    wait_count(eng, mixed, TPB * (row - 1))
                    eng.tensor_scalar(onehot[k % 2][0:PATCHES, :], p_in[k][:], 1.0, rank[:], ALU.max, ALU.is_equal).then_inc(onehot_ready, 1)

                def lo_pool(row, k):
                    eng.wait_ge(pool_hi_ready, row + 1)
                    eng.tensor_tensor(pool_lo[k % 2][:], ps_d[0:ROWS, :], pool_hi[k % 2][:].bitcast(F32), ALU.subtract).then_inc(pool_lo_ready, 1)

                def lo_tile(n, j):
                    eng.wait_ge(hi_ready, n + 1)
                    eng.tensor_tensor(xt_lo[j][:], ps_t[j][:], xt_hi[j][:].bitcast(F32), ALU.subtract).then_inc(lo_ready, 1)

                def add_tile(n, g, k, t):
                    if t == 0:
                        wait_count(eng, x1_stored[k], DMA * g)
                    eng.wait_ge(mixed, n + 1)
                    eng.scalar_tensor_tensor(x1[k][:, t, :], ps_o[t % 2][:], gate[:], x_in[k][:, t, :],
                                             ALU.mult, ALU.add).then_inc(x1_ready, 1)

                def r_stat(r, k, t):
                    eng.wait_ge(x1_ready, TPB * r + t + 1)
                    eng.bn_stats(r_stats[k % 2][:, t, :], x1[k][:, t, :]).then_inc(r_stats_done, 1)

                def r_spreads(r, k):
                    hold(eng, r_stats_done, TPB * (r + 1), passed)
                    for t in range(TPB):
                        eng.bn_aggr(r_moments[k % 2][:, t, :], r_stats[k % 2][:, t, :]).then_inc(r_moments_done, 1)
                    eng.wait_ge(r_moments_done, TPB * (r + 1))
                    eng.tensor_scalar(r_spread[k % 2][:], r_moments[k % 2][:, :, 1], EPS, None, ALU.add).then_inc(r_spread_ready, 1)

                def r_shifts(r, k):
                    eng.wait_ge(r_scale_ready, r + 1)
                    eng.scalar_tensor_tensor(r_shift[k % 2][:], r_moments[k % 2][:, :, 0], -1.0, r_scale[k % 2][:],
                                             ALU.mult, ALU.mult).then_inc(r_shift_ready, 1)

                class Steps:
                    done = 0

                    def then(self, ins):
                        self.done += 1
                        ins.then_inc(step, 1)

                    def settle(self, r):
                        hold(eng, step, STEPS * r + self.done, passed)

                own = Steps()
                spread_out = lambda ap: ap.unsqueeze(2).broadcast_to([P, TOP_K * TPB, EXPERTS])

                def choose(r, k):
                    own.done = 0
                    eng.wait_ge(scored, TPB * (r + 1))
                    eng.tensor_tensor(logits[:], ps_s[:].rearrange("p (t e) -> p t e", e=EXPERTS),
                                      router_b[:].unsqueeze(1).broadcast_to([P, TPB, EXPERTS]), ALU.add).then_inc(logits_ready, 1)
                    hold(eng, logits_ready, r + 1, passed)
                    for t in range(TPB):
                        own.then(eng.max(top[:, t, :], logits[:, t, :]))
                    own.settle(r)
                    for t in range(TPB):
                        own.then(eng.max_index(top_at[:, t, :], top[:, t, :], logits[:, t, :]))
                    eng.tensor_tensor(gap[:], top[:, :, 1], top[:, :, 0], ALU.subtract).then_inc(gap_ready, 1)
                    own.settle(r)
                    own.then(eng.tensor_copy(choice[:], top_at[:, :, 0:TOP_K].rearrange("p t k -> p k t")))
                    own.settle(r)
                    own.then(eng.tensor_tensor(chosen[:], expert_id[:].unsqueeze(1).broadcast_to([P, TOP_K * TPB, EXPERTS]),
                                               spread_out(choice[:].rearrange("p k t -> p (k t)")), ALU.is_equal))
                    own.settle(r)
                    eng.tensor_tensor(either[:], chosen[:, 0:TPB, :].rearrange("p t e -> p (t e)"),
                                      chosen[:, TPB:, :].rearrange("p t e -> p (t e)"), ALU.add).then_inc(either_ready, 1)

                def find_places(r, k):
                    eng.wait_ge(counted, r + 1)
                    own.then(eng.tensor_tensor(place[:], ps_p[:, 0:TPB * EXPERTS].rearrange("p (t e) -> p t e", e=EXPERTS),
                                               taken[:].unsqueeze(1).broadcast_to([P, TPB, EXPERTS]), ALU.add))
                    own.settle(r)
                    eng.tensor_tensor(taken[:], taken[:], ps_p[:, TPB * EXPERTS:], ALU.add).then_inc(taken_ready, 1)
                    own.then(eng.tensor_tensor(picked[:].rearrange("p (k t) e -> p k t e", k=TOP_K), chosen[:].rearrange("p (k t) e -> p k t e", k=TOP_K),
                                               place[:].unsqueeze(1).broadcast_to([P, TOP_K, TPB, EXPERTS]), ALU.mult))
                    own.settle(r)
                    own.then(eng.tensor_reduce(own_place[:], picked[:], AX_X, ALU.add))
                    own.settle(r)

                def make_entries(r, k):
                    flat_choice = choice[:].rearrange("p k t -> p (k t)")
                    own.then(eng.tensor_scalar(past[:], own_place[:], float(CAPACITY), float(FAR), ALU.is_ge, ALU.mult))
                    own.then(eng.scalar_tensor_tensor(slot_f[:], flat_choice, float(CAPACITY), own_place[:], ALU.mult, ALU.add))
                    eng.wait_ge(second_ready, r + 1)
                    own.then(eng.tensor_scalar(total[:], second[:], 1.0, None, ALU.add))
                    own.settle(r)
                    own.then(eng.tensor_tensor(slot[k][:], slot_f[:], past[:], ALU.add))
                    own.then(eng.reciprocal(total[:], total[:]))
                    own.settle(r)
                    own.then(eng.tensor_scalar(rows[k][:, :, WEIGHT], total[:], ffn_gate[:], None, ALU.mult))
                    own.then(eng.tensor_copy(rows[k][:, :, TOKEN].bitcast(I32), token[:]))
                    own.then(eng.tensor_copy(rows[k][:, :, CHOICE:CHOICE + TOP_K], choice[:].rearrange("p k t -> p t k")))
                    own.settle(r)
                    own.then(eng.tensor_scalar(token[:], token[:], float(SEQ), None, ALU.add))
                    eng.tensor_tensor(rows[k][:, :, WEIGHT + 1], rows[k][:, :, WEIGHT], second[:], ALU.mult).then_inc(routed, 1)
                    assert own.done == STEPS, own.done

                def raise_flag(g):
                    eng.wait_ge(taken_ready, GROUP * g)
                    eng.tensor_reduce(least[:], taken[:], AX_X, ALU.min).then_inc(least_ready, 1)
                    eng.wait_ge(least_ready, g)
                    eng.tensor_scalar(active[:], least[:], float(CAPACITY), None, ALU.is_lt).then_inc(flag_ready, 1)

                def route_step(b, k, t):
                    if there(b - 1):
                        r_stat(b - 1, (k - 1) % GROUP, t)
                    if t == 0 and there(b - 2):
                        r_shifts(b - 2, (k - 2) % GROUP)
                    if there(b - 3):
                        if t > 0:
                            (choose, find_places, make_entries)[t - 1](b - 3, (k - 3) % GROUP)
                    if t == TPB - 1 and there(b - 1):
                        r_spreads(b - 1, (k - 1) % GROUP)

                eng.wait_ge(marks_loaded, 4 * DMA)
                eng.wait_ge(const_set, 4)
                eng.tensor_copy(lens[:], lens_i[:]).then_inc(prep, 1)
                eng.wait_ge(prep, 1)
                own_ends = ends[:, 0:PATCHES]
                eng.tensor_tensor_scan(own_ends, lens[:], nothing[:], -1.0, ALU.add, ALU.add).then_inc(prep, 1)
                eng.wait_ge(prep, 2)
                eng.tensor_scalar(wraps[:], own_ends, 0.0, float(SEQ), ALU.is_lt, ALU.mult).then_inc(prep, 1)
                eng.wait_ge(prep, 3)
                eng.tensor_tensor(own_ends, own_ends, wraps[:], ALU.add).then_inc(ends_ready, 1)
                eng.wait_ge(ends_ready, 1)

                def mark(p, i):
                    wait_count(eng, mark_added, p - MARKS + 1)
                    eng.tensor_scalar(is_end[i][:], pos[:], ends[:, bass.ds(p, 1)], None, ALU.is_equal).then_inc(marked, 1)

                def mark_turn(m):
                    for i in range(MARKS):
                        mark(MARKS * m + i, i)

                mark_turn(0)
                with eng.Fori(1, 3) as m:
                    mark_turn(m)
                stats(0, 1, 0, range(TPB))
                spreads(0, 0)
                mark_turn(3)
                shifts(0, 0)
                eng.wait_ge(const_loaded, CONSTS)
                patches(0, 0)
                eng.wait_ge(decay_hi_ready, 1)
                eng.tensor_tensor(decay_lo[:], decay[:], decay_hi[:].bitcast(F32), ALU.subtract).then_inc(decay_lo_ready, 1)
                with eng.Fori(4, ROWS // MARKS) as m:
                    mark_turn(m)
                lo_tile(0, 0)
                eng.wait_ge(mark_added, ROWS)
                eng.tensor_scalar(marks[:], ps_m[:, 0:SEQ // 2], 1.0, None, ALU.min).then_inc(prep, 1)
                eng.wait_ge(prep, 4)
                eng.tensor_tensor_scan(ended[:], marks[:], marks[:], 0.0, ALU.add, ALU.max).then_inc(ended_ready, 1)
                eng.wait_ge(ended_ready, 1)
                eng.wait_ge(carried, 1)
                eng.tensor_scalar(plug[:], ended[:], ps_c[:, 0:1], None, ALU.add).then_inc(plug_ready, 1)
                lo_pool(0, 0)
                lo_tile(1, 1)
                stats(1, 1, 1, range(TPB))
                spreads(1, 1)
                shifts(1, 1)
                eng.wait_ge(gate_ready, 2)
                onehots(0, 1, 0)

                def turn(g, routing, last):
                    for k in range(GROUP):
                        b = GROUP * g + k
                        nk, ak = (k + 1) % GROUP, (k + 2) % GROUP
                        end = last and k == GROUP - 1
                        for t in range(TPB):
                            n = TPB * b + t
                            if not (end and t == TPB - 1) and not (isinstance(n, int) and n == 0):
                                lo_tile(n + 1, (t + 1) % 2)
                            if not (last and k >= GROUP - 2):
                                stats(b + 2, g + 1 + (k + 2) // GROUP, ak, (t,))
                            if t == 0 and not end and not (isinstance(b, int) and b == 0):
                                shifts(b + 1, nk)
                            if t == 0 and not end:
                                patches(b + 1, nk)
                                onehots(b + 1, g + 1 + (k + 1) // GROUP, nk)
                            if routing:
                                if t == 1 and k == GROUP - 1 and not (isinstance(g, int) and g == 0):
                                    raise_flag(g)
                                route_step(b, k, t)
                            if t == TPB - 1:
                                if not (last and k >= GROUP - 2):
                                    spreads(b + 2, ak)
                                if not end:
                                    lo_pool(b + 1, nk)
                            add_tile(n, g, k, t)
                    if routing and not (isinstance(g, int) and g == 0):
                        hold(eng, flag_ready, g, passed)

                def after(b, k):
                    for t in range(TPB):
                        route_step(b, k, t)

                def free_slots():
                    eng.wait_ge(taken_ready, BATCH)
                    eng.tensor_tensor(is_taken[:], list_place[:].unsqueeze(1).broadcast_to([P, EXPERTS, ET]),
                                      taken[:].unsqueeze(2).broadcast_to([P, EXPERTS, ET]), ALU.is_lt).then_inc(taken_compared, 1)
                    eng.wait_ge(taken_compared, 1)
                    eng.scalar_tensor_tensor(free_slot[:], is_taken[:].rearrange("p e t -> p (e t)"), float(FAR), list_slot[:],
                                             ALU.mult, ALU.add).then_inc(free_ready, 1)

                turns(eng, turn, after, free_slots)


def experts(nc, io, x1_dram, tokens_dram, shared):
    W_out = io["W_out"]
    x1_rows = x1_dram.rearrange("b s d -> (b s) d")
    tok_rows = tokens_dram.rearrange("(e p t) d -> e p t d", e=EXPERTS, t=ET)
    meta = tokens_dram.rearrange("(e p t) d -> e p t d", e=EXPERTS, t=ET)[:, :, :, D:ROW]
    HALF = CAPACITY // 2
    with ExitStack() as ctx:
        def sb(name, shape, dt=F32):
            return ctx.enter_context(nc.sbuf_tensor(name, shape, dt))

        def ps(name, shape):
            return ctx.enter_context(nc.psum_tensor(name, shape, F32))

        def sem(name):
            return ctx.enter_context(nc.semaphore(name))

        eye = shared.eye
        lists = sb("lists", [P, EXPERTS, ET * META])
        list_expert = sb("list_expert", [P, EXPERTS * ET])
        is_own = sb("is_own", [P, TOP_K, EXPERTS * ET])
        own_w = sb("own_w", [P, EXPERTS * ET])
        this_ids = sb("this_ids", [P, ET], I32)
        this_w = sb("this_w", [P, ET])
        h_hi = sb("h_hi", [P, HC, CAPACITY], F32R)
        h_lo = sb("h_lo", [P, HC, CAPACITY], F32R)
        t_hi = sb("t_hi", [P, KC, CAPACITY], F32R)
        t_lo = sb("t_lo", [P, KC, CAPACITY], F32R)
        o_hi = sb("o_hi", [P, HC, D], F32R)
        o_lo = sb("o_lo", [P, HC, D], F32R)
        o_raw = [sb(f"o_raw{i}", [P, D]) for i in range(4)]
        wv_raw = [shared.weights[:].rearrange("p (m c h) -> p m c h", m=2, c=KC), sb("wv_raw1", [P, 2, KC, QC * P])[:]]
        wv_hi = [sb(f"wv_hi{i}", [P, 2, KC, P], F32R) for i in range(2)]
        wv_lo = [sb(f"wv_lo{i}", [P, 2, KC, P], F32R) for i in range(2)]
        silu = [sb(f"silu{i}", [P, HALF]) for i in range(2)]
        prod = [sb(f"prod{i}", [P, HALF]) for i in range(2)]
        tok = [sb(f"tok{i}", [P, D]) for i in range(4)]
        acc = [sb(f"acc{i}", [P, D]) for i in range(4)]
        new = [sb(f"new{i}", [P, D]) for i in range(2)]

        ps_g = [ps(f"ps_g{i}", [P, HALF]) for i in range(2)]
        ps_a = [ps(f"ps_a{i}", [P, HALF]) for i in range(2)]
        ps_y = [ps(f"ps_y{i}", [P, D]) for i in range(2)]
        ps_t = [ps(f"e_ps_t{i}", [P, D]) for i in range(2)]

        const_loaded = sem("e_const_loaded")
        CONSTS = (1 + EXPERTS) * DMA
        cleared = sem("cleared")
        wv_loaded = [shared.first_loaded, sem("wv_loaded1")]
        o_loaded = [sem(f"o_loaded{i}") for i in range(4)]
        ids_ready = sem("ids_ready")
        weights_ready = sem("weights_ready")
        own_steps = sem("own_steps")
        tok_loaded = [sem(f"tok_loaded{i}") for i in range(4)]
        acc_gathered = [sem(f"acc_gathered{i}") for i in range(4)]
        scattered = [sem(f"scattered{i}") for i in range(2)]
        wv_hi_ready = sem("wv_hi_ready")
        wv_lo_ready = sem("wv_lo_ready")
        o_hi_ready = sem("o_hi_ready")
        o_lo_ready = sem("o_lo_ready")
        gated = sem("gated")
        raised = sem("raised")
        silu_ready = sem("silu_ready")
        prod_ready = sem("prod_ready")
        h_hi_ready = sem("h_hi_ready")
        h_lo_ready = sem("h_lo_ready")
        turned = sem("e_turned")
        t_hi_ready = sem("t_hi_ready")
        t_lo_ready = sem("t_lo_ready")
        lowered = sem("lowered")
        new_ready = sem("new_ready")
        passed = sem("passed")

        def loop(eng, body):
            body(0, False)
            with eng.Fori(1, EXPERTS - 1) as e:
                body(e, False)
            body(EXPERTS - 1, True)

        with nc.Block() as block:

            @block.sync
            def _(eng):
                def load_tile(e, t):
                    wait_count(eng, turned, ET * e + t - 3)
                    eng.dma_start(tok[t % 4][:], tok_rows[e][:, t, 0:D]).then_inc(tok_loaded[t % 4], DMA)

                def load_weights(e, q):
                    i = q % 2
                    quarter = HC // QC * e + q
                    if not isinstance(e, int) or quarter > 0:
                        wait_count(eng, wv_hi_ready, QC * (quarter - 1))
                        wait_count(eng, wv_lo_ready, QC * (quarter - 1))
                        load_quarter(eng, io, wv_raw[i], e, q, wv_loaded[i])
                    for h in range(QC * q, QC * (q + 1)):
                        wait_count(eng, o_hi_ready, HC * e + h - 3)
                        wait_count(eng, o_lo_ready, HC * e + h - 3)
                        eng.dma_start(o_raw[h % 4][:], W_out[e][h * P:(h + 1) * P, :]).then_inc(o_loaded[h % 4], DMA)

                for t in range(ET):
                    load_tile(0, t)
                load_weights(0, 0)
                eng.dma_start(list_expert[:], io["c_list_expert"]).then_inc(const_loaded, DMA)
                for e in range(EXPERTS):
                    eng.dma_start(lists[:, e].rearrange("p (t w) -> p t w", w=META), meta[e]).then_inc(const_loaded, DMA)

                def body(e, last):
                    for q in range(1, HC // QC):
                        load_weights(e, q)
                    if not last:
                        load_weights(e + 1, 0)
                        for t in range(ET):
                            load_tile(e + 1, t)

                loop(eng, body)

            @block.gpsimd
            def _(eng):
                bound = dict(bounds_check=TOKENS - 1, oob_is_err=False)

                def gather_acc(n, t, first):
                    if not first:
                        hold(eng, new_ready, n - 3, passed)
                    eng.indirect_dma_start(acc[t % 4][:], None, x1_rows, bass.IndirectOffsetOnAxis(this_ids[:, t:t + 1], 0),
                                           **bound).then_inc(acc_gathered[t % 4], DMA)

                def scatter(n, t):
                    hold(eng, new_ready, n + 1, passed)
                    eng.indirect_dma_start(x1_rows, bass.IndirectOffsetOnAxis(this_ids[:, t:t + 1], 0), new[t % 2][:], None,
                                           **bound).then_inc(scattered[t % 2], DMA)

                eng.wait_ge(const_loaded, CONSTS)
                eng.wait_ge(cleared, 1)
                for i in range(GROUP):
                    eng.wait_ge(shared.x1_stored[i], DMA * (BATCH // GROUP + (i == GROUP - 1)))

                def body(e, last):
                    own = lists[:, bass.ds(e, 1), :].rearrange("p o (t w) -> p (o t) w", w=META)[:, :, TOKEN - D].bitcast(I32)
                    for i in range(2):
                        if not isinstance(e, int) or e > 0:
                            hold(eng, scattered[i], DMA * (ET // 2) * e, passed)
                    eng.tensor_copy(this_ids[:], own).then_inc(ids_ready, 1)
                    hold(eng, ids_ready, e + 1, passed)
                    for t in range(4):
                        gather_acc(ET * e + t, t, isinstance(e, int) and e == 0)
                    for t in range(ET):
                        scatter(ET * e + t, t)
                        if t + 4 < ET:
                            gather_acc(ET * e + t + 4, t + 4, False)

                loop(eng, body)
                for i in range(2):
                    eng.wait_ge(scattered[i], DMA * (ET // 2) * EXPERTS)

            @block.tensor
            def _(eng):
                def turn_tile(n, turn_no, t):
                    eng.wait_ge(tok_loaded[t % 4], DMA * (2 * turn_no + t // 4 + 1))
                    wait_count(eng, t_hi_ready, n - 1)
                    wait_count(eng, t_lo_ready, n - 1)
                    for c in range(KC):
                        mm = eng.transpose(ps_t[t % 2][:, c * P:(c + 1) * P], tok[t % 4][:, c * P:(c + 1) * P], eye[:])
                    mm.then_inc(turned, 1)

                def product(out, stationary, moving, i, first, last):
                    (s_hi, s_lo), (m_hi, m_lo) = stationary, moving
                    eng.matmul(out, s_hi, m_hi, start=first, stop=False)
                    eng.matmul(out, s_hi, m_lo, start=False, stop=False)
                    return eng.matmul(out, s_lo, m_hi, start=False, stop=last)

                def raise_half(out, m, i, half):
                    cols = slice(half * HALF, (half + 1) * HALF)
                    for c in range(KC):
                        mm = product(out, (wv_hi[i][:, m, c, :], wv_lo[i][:, m, c, :]),
                                     (t_hi[:, c, cols], t_lo[:, c, cols]), c, c == 0, c == KC - 1)
                    return mm

                for t in range(ET // 2):
                    turn_tile(t, 0, t)

                def body(e, last):
                    very_first = isinstance(e, int) and e == 0
                    if not very_first:
                        eng.wait_ge(t_hi_ready, ET * (e + 1))
                        eng.wait_ge(t_lo_ready, ET * (e + 1))
                    for h in range(HC):
                        chunk = HC * e + h
                        eng.wait_ge(wv_hi_ready, chunk + 1)
                        eng.wait_ge(wv_lo_ready, chunk + 1)
                        for s in range(2):
                            if very_first and h == 0:
                                eng.wait_ge(t_hi_ready, ET // 2 * (s + 1))
                                eng.wait_ge(t_lo_ready, ET // 2 * (s + 1))
                            wait_count(eng, silu_ready, 2 * chunk + s - 1)
                            raise_half(ps_g[s][:], 1, h % 2, s).then_inc(gated, 1)
                            if very_first and h == 0 and s == 0:
                                for t in range(ET // 2, ET):
                                    turn_tile(t, 0, t)
                            wait_count(eng, prod_ready, 2 * chunk + s - 1)
                            raise_half(ps_a[s][:], 0, h % 2, s).then_inc(raised, 1)
                    for t in range(ET):
                        if not last:
                            turn_tile(ET * (e + 1) + t, e + 1, t)
                        wait_count(eng, new_ready, ET * e + t - 1)
                        rows = slice(t * P, (t + 1) * P)
                        for h in range(HC):
                            if t == 0:
                                eng.wait_ge(h_hi_ready, 2 * (HC * e + h) + 1)
                                eng.wait_ge(h_lo_ready, 2 * (HC * e + h) + 1)
                                eng.wait_ge(o_hi_ready, HC * e + h + 1)
                                eng.wait_ge(o_lo_ready, HC * e + h + 1)
                            if t == ET // 2 and h == 0:
                                eng.wait_ge(h_hi_ready, 2 * HC * (e + 1))
                                eng.wait_ge(h_lo_ready, 2 * HC * (e + 1))
                            mm = product(ps_y[t % 2][:], (h_hi[:, h, rows], h_lo[:, h, rows]),
                                         (o_hi[:, h, :], o_lo[:, h, :]), h, h == 0, h == HC - 1)
                        mm.then_inc(lowered, 1)

                loop(eng, body)

            @block.scalar
            def _(eng):
                def split_wv(chunk, quarter_turn, h):
                    q = h // QC
                    eng.wait_ge(wv_loaded[q % 2], 2 * DMA * (2 * quarter_turn + q // 2 + 1))
                    wait_count(eng, raised, 2 * (chunk - 1))
                    cols = slice(h % QC * P, (h % QC + 1) * P)
                    eng.activation(wv_hi[h % 2][:].rearrange("p m c h -> p (m c) h"), wv_raw[q % 2][:, :, :, cols].rearrange("p m c h -> p (m c) h"),
                                   ACT.Copy).then_inc(wv_hi_ready, 1)

                def split_list_tile(e, t):
                    eng.wait_ge(turned, ET * e + t + 1)
                    if t == 0:
                        wait_count(eng, raised, 2 * HC * e)
                    eng.activation(t_hi[:, :, t * P:(t + 1) * P], ps_t[t % 2][:].rearrange("p (c s) -> p c s", c=KC),
                                   ACT.Copy).then_inc(t_hi_ready, 1)

                split_wv(0, 0, 0)
                for t in range(ET):
                    split_list_tile(0, t)

                def body(e, last):
                    for h in range(HC):
                        chunk = HC * e + h
                        if h + 1 < HC:
                            split_wv(chunk + 1, e, h + 1)
                        elif not last:
                            split_wv(chunk + 1, e + 1, 0)
                        eng.wait_ge(o_loaded[h % 4], DMA * (2 * e + h // 4 + 1))
                        if h == 0:
                            wait_count(eng, lowered, ET * e)
                        eng.activation(o_hi[:, h, :], o_raw[h % 4][:], ACT.Copy).then_inc(o_hi_ready, 1)
                        for s in range(2):
                            eng.wait_ge(gated, 2 * chunk + s + 1)
                            wait_count(eng, prod_ready, 2 * chunk + s - 1)
                            eng.activation(silu[s][:], ps_g[s][:], ACT.Silu).then_inc(silu_ready, 1)
                            eng.wait_ge(prod_ready, 2 * chunk + s + 1)
                            eng.activation(h_hi[:, h, s * HALF:(s + 1) * HALF], prod[s][:], ACT.Copy).then_inc(h_hi_ready, 1)
                    if not last:
                        for t in range(ET):
                            split_list_tile(e + 1, t)

                loop(eng, body)

            @block.vector
            def _(eng):
                def split_wv(chunk, h):
                    q = h // QC
                    eng.wait_ge(wv_hi_ready, chunk + 1)
                    cols = slice(h % QC * P, (h % QC + 1) * P)
                    eng.tensor_tensor(wv_lo[h % 2][:].rearrange("p m c h -> p (m c) h"), wv_raw[q % 2][:, :, :, cols].rearrange("p m c h -> p (m c) h"),
                                      wv_hi[h % 2][:].bitcast(F32).rearrange("p m c h -> p (m c) h"), ALU.subtract).then_inc(wv_lo_ready, 1)

                def split_list_tile(e, t):
                    cols = slice(t * P, (t + 1) * P)
                    eng.wait_ge(t_hi_ready, ET * e + t + 1)
                    eng.tensor_tensor(t_lo[:, :, cols], ps_t[t % 2][:].rearrange("p (c s) -> p c s", c=KC),
                                      t_hi[:, :, cols].bitcast(F32), ALU.subtract).then_inc(t_lo_ready, 1)

                split_wv(0, 0)
                for t in range(ET):
                    split_list_tile(0, t)
                for i in range(3):
                    eng.memset(acc[i][:], 0.0)
                eng.memset(acc[3][:], 0.0).then_inc(cleared, 1)
                eng.wait_ge(const_loaded, CONSTS)
                word = lists[:].rearrange("p e (t w) -> p (e t) w", w=META)
                for i in range(TOP_K):
                    eng.tensor_tensor(is_own[:, i], word[:, :, CHOICE - D + i], list_expert[:], ALU.is_equal).then_inc(own_steps, 1)
                for i in range(TOP_K):
                    eng.wait_ge(own_steps, i + 1)
                    eng.tensor_tensor(is_own[:, i], is_own[:, i], word[:, :, WEIGHT - D + i], ALU.mult).then_inc(own_steps, 1)
                eng.wait_ge(own_steps, 2 * TOP_K)
                eng.tensor_tensor(own_w[:], is_own[:, 0], is_own[:, 1], ALU.add).then_inc(own_steps, 1)
                eng.wait_ge(own_steps, 2 * TOP_K + 1)

                def body(e, last):
                    if not isinstance(e, int) or e > 0:
                        hold(eng, new_ready, ET * e, passed)
                    eng.tensor_copy(this_w[:], own_w[:, bass.ds(e * ET, ET)]).then_inc(weights_ready, 1)
                    for h in range(HC):
                        chunk = HC * e + h
                        if h + 1 < HC:
                            split_wv(chunk + 1, h + 1)
                        elif not last:
                            split_wv(chunk + 1, 0)
                        eng.wait_ge(o_hi_ready, chunk + 1)
                        eng.tensor_tensor(o_lo[:, h, :], o_raw[h % 4][:], o_hi[:, h, :].bitcast(F32), ALU.subtract).then_inc(o_lo_ready, 1)
                        for s in range(2):
                            cols = slice(s * HALF, (s + 1) * HALF)
                            eng.wait_ge(silu_ready, 2 * chunk + s + 1)
                            eng.wait_ge(raised, 2 * chunk + s + 1)
                            wait_count(eng, h_hi_ready, 2 * chunk + s - 1)
                            eng.tensor_tensor(prod[s][:], ps_a[s][:], silu[s][:], ALU.mult).then_inc(prod_ready, 1)
                            eng.wait_ge(h_hi_ready, 2 * chunk + s + 1)
                            eng.tensor_tensor(h_lo[:, h, cols], prod[s][:], h_hi[:, h, cols].bitcast(F32), ALU.subtract).then_inc(h_lo_ready, 1)
                    eng.wait_ge(weights_ready, e + 1)
                    for t in range(ET):
                        if not last:
                            split_list_tile(e + 1, t)
                        eng.wait_ge(acc_gathered[t % 4], DMA * (2 * e + t // 4 + 1))
                        wait_count(eng, scattered[t % 2], DMA * (ET // 2 * e + t // 2))
                        eng.wait_ge(lowered, ET * e + t + 1)
                        eng.scalar_tensor_tensor(new[t % 2][:], ps_y[t % 2][:], this_w[:, t:t + 1], acc[t % 4][:],
                                                 ALU.mult, ALU.add).then_inc(new_ready, 1)

                loop(eng, body)


def kernel(**inputs):
    from concourse import bacc
    from concourse.bass_utils import run_bass_kernel_spmd

    x = np.asarray(inputs["x"])
    laid_out = {
        "x": x,
        "ctx": np.asarray(inputs["ctx_2048"]),
        "lens": np.asarray(inputs["mask_BxS2_if0"]),
        "g_xattn": np.asarray(inputs["g_xattn"]),
        "g_ffn": np.asarray(inputs["g_ffn"]),
        "w_in": np.asarray(inputs["L0_xattn_W_in"]).T,
        "b_in": np.asarray(inputs["L0_xattn_b_in"]).reshape(1, D),
        "gain_res": np.asarray(inputs["L0_xattn_g_res"]).reshape(KC, P).T,
        "gain_ctx": np.asarray(inputs["L0_xattn_g_init"]),
        "router_w": np.asarray(inputs["L0_ffn_router_w"]).T,
        "router_b": np.asarray(inputs["L0_ffn_router_b"]),
        "W": np.asarray(inputs["L0_ffn_W"]),
        "V": np.asarray(inputs["L0_ffn_V"]),
        "W_out": np.asarray(inputs["L0_ffn_W_out"]),
        **constants(),
    }
    nc = bacc.Bacc("TRN2", target_bir_lowering=False, num_devices=1)
    arrays, io = {}, {}
    for name, a in laid_out.items():
        arrays[f"in_{name}"] = np.ascontiguousarray(a)
        io[name] = nc.dram_tensor(f"in_{name}", a.shape, mybir.dt.from_np(a.dtype), kind="ExternalInput").ap()
    out = nc.dram_tensor("out_x", [BATCH, SEQ, D], F32, kind="ExternalOutput").ap()
    build(nc, io, out)
    result = run_bass_kernel_spmd(nc, [arrays], core_ids=[0])
    return result.results[0]["out_x"]


def build(nc, io, out):
    tokens_dram = nc.dram_tensor("tokens_dram", [EXPERTS * CAPACITY, ROW], F32, kind="Internal").ap()
    with ExitStack() as ctx:
        shared = Shared(nc, ctx)
        mix(nc, io, out, tokens_dram, shared)
        experts(nc, io, out, tokens_dram, shared)
```
